# Optimizing a Trainium2 kernel written in Bass

```python
import numpy as np
import jax
import jax.numpy as jnp

def _softmax(x, axis=-1):
    return jax.nn.softmax(x, axis=axis)

def _gelu(x):
    return jax.nn.gelu(x, approximate=True)

def _silu(x):
    return jax.nn.silu(x)

def _sigmoid(x):
    return jax.nn.sigmoid(x)

def _layernorm(x, axis=-1, eps=1e-05):
    m = jnp.mean(x, axis=axis, keepdims=True)
    v = jnp.var(x, axis=axis, keepdims=True)
    return (x - m) / jnp.sqrt(v + eps)

def _scatter_add(tgt, idx, src, axis=0):
    return tgt.at[idx].add(src)

def _segment_sum(src, seg, n):
    return jax.ops.segment_sum(src, seg, n)
kernel_name = 'mk_prb_d2_jaxref_r8_47ad6b'

def setup_inputs(seed: int=0):
    np.random.seed(seed)
    _w = jnp.asarray

    def _L0_attn_setup():
        import jax, jax.numpy as jnp
        import numpy as np
        N_HEADS = 16
        N_KV_HEADS = 4
        WINDOW = 64
        N_META = 16
        ROPE_BASE = 10000.0

        def rotate_half(x):
            x1 = x[..., 0::2]
            x2 = x[..., 1::2]
            return jnp.stack((-x2, x1), axis=-1).reshape(x.shape)

        def apply_rope(x, positions):
            d = x.shape[-1]
            inv_freq = 1.0 / ROPE_BASE ** (jnp.arange(0, d, 2, dtype=jnp.float32) / d)
            angles = positions.astype(jnp.float32)[:, None] * inv_freq
            cos = jnp.repeat(jnp.cos(angles), 2, axis=-1)[None, None]
            sin = jnp.repeat(jnp.sin(angles), 2, axis=-1)[None, None]
            return x * cos + rotate_half(x) * sin
        key = jax.random.key(seed)
        ks = jax.random.split(key, 4)
        B, S, E = (2, 512, 256)
        hd = E // N_HEADS
        kv_out = 2 * N_KV_HEADS * hd
        sc = 1.0 / np.sqrt(E).astype(np.float32)
        return {'x': jax.random.normal(ks[0], (B, S, E), jnp.float32), 'Wq': jax.random.normal(ks[1], (E, E), jnp.float32) * sc, 'bq': jnp.zeros((E,), jnp.float32), 'Wkv': jax.random.normal(ks[2], (E, kv_out), jnp.float32) * sc, 'bkv': jnp.zeros((kv_out,), jnp.float32), 'Wo': jax.random.normal(ks[3], (E, E), jnp.float32) * sc, 'bo': jnp.zeros((E,), jnp.float32)}
    _L0_attn_in = _L0_attn_setup()

    def _L0_ffn_setup():
        import jax, jax.numpy as jnp
        import numpy as np
        TOP_K = 8
        CAPACITY = 128
        key = jax.random.key(seed)
        k1, k2, k3, k4 = jax.random.split(key, 4)
        B, S, H, E, I = (2, 128, 256, 64, 96)
        hidden_states = jax.random.normal(k1, (B, S, H), dtype=jnp.float32)
        router_weight = jax.random.normal(k2, (E, H), dtype=jnp.float32) * 0.02
        gate_up_proj = jax.random.normal(k3, (E, H, 2 * I), dtype=jnp.float32) * 0.02
        down_proj = jax.random.normal(k4, (E, I, H), dtype=jnp.float32) * 0.02
        return {'hidden_states': hidden_states, 'router_weight': router_weight, 'gate_up_proj': gate_up_proj, 'down_proj': down_proj}
    _L0_ffn_in = _L0_ffn_setup()

    def _L1_attn_setup():
        import jax, jax.numpy as jnp
        import numpy as np
        BLOCK = 32
        key = jax.random.key(seed)
        ks = jax.random.split(key, 6)
        b, n, hid = (2, 512, 256)
        h, d = (16, 128)
        x = jax.random.normal(ks[0], (b, n, hid), dtype=jnp.float32)
        slope_rate = jax.random.uniform(ks[1], (h, 1, 1), dtype=jnp.float32)
        Wqkv = jax.random.normal(ks[2], (3 * h * d, hid), dtype=jnp.float32) * 0.02
        Wg = jax.random.normal(ks[3], (h * d, hid), dtype=jnp.float32) * 0.02
        norm_w = jnp.ones((h * d,), dtype=jnp.float32)
        Wo = jax.random.normal(ks[4], (hid, h * d), dtype=jnp.float32) * 0.02
        return {'x': x, 'slope_rate': slope_rate, 'Wqkv': Wqkv, 'Wg': Wg, 'norm_w': norm_w, 'Wo': Wo}
    _L1_attn_in = _L1_attn_setup()

    def _L1_ffn_setup():
        import jax, jax.numpy as jnp
        import numpy as np
        B, S, D, F, E, K = (2, 256, 256, 512, 8, 1)

        def _silu_mul(gu):
            g, u = jnp.split(gu, 2, axis=-1)
            return jax.nn.silu(g) * u

        def _moe_forward(hidden_states, router_w, w_gate_up, w_down, shared_gate_up, shared_down, top_k=K):
            b, s, d = hidden_states.shape
            x = hidden_states.reshape(-1, d)
            router_logits = x @ router_w.T
            topk_vals, topk_ids = jax.lax.top_k(router_logits, top_k)
            gate = jax.nn.sigmoid(topk_vals.astype(jnp.float32)).astype(x.dtype)
            xs = (x[:, None, :] * gate[:, :, None]).reshape(-1, d)
            ids_flat = topk_ids.reshape(-1)
            n_experts = w_gate_up.shape[0]

            def body(acc, inp):
                wg, wd, e = inp
                h = _silu_mul(xs @ wg)
                o = h @ wd
                mask = (ids_flat == e)[:, None]
                return (acc + jnp.where(mask, o, jnp.zeros((), o.dtype)), None)
            acc0 = jnp.zeros_like(xs)
            routed, _ = jax.lax.scan(body, acc0, (w_gate_up, w_down, jnp.arange(n_experts)))
            routed = routed.reshape(-1, top_k, d).sum(1)
            shared = _silu_mul(x @ shared_gate_up) @ shared_down
            return (routed + shared).reshape(b, s, d)
        key = jax.random.key(seed)
        ks = jax.random.split(key, 6)
        scale = 0.02
        return {'hidden_states': jax.random.normal(ks[0], (B, S, D), jnp.float32), 'router_w': jax.random.normal(ks[1], (E, D), jnp.float32) * scale, 'w_gate_up': jax.random.normal(ks[2], (E, D, 2 * F), jnp.float32) * scale, 'w_down': jax.random.normal(ks[3], (E, F, D), jnp.float32) * scale, 'shared_gate_up': jax.random.normal(ks[4], (D, 2 * F), jnp.float32) * scale, 'shared_down': jax.random.normal(ks[5], (F, D), jnp.float32) * scale}
    _L1_ffn_in = _L1_ffn_setup()
    _d = {'L0_attn_x': _L0_attn_in['x'], 'L0_attn_Wq': _L0_attn_in['Wq'], 'L0_attn_bq': _L0_attn_in['bq'], 'L0_attn_Wkv': _L0_attn_in['Wkv'], 'L0_attn_bkv': _L0_attn_in['bkv'], 'L0_attn_Wo': _L0_attn_in['Wo'], 'L0_attn_bo': _L0_attn_in['bo'], 'L0_ffn_router_weight': _L0_ffn_in['router_weight'], 'L0_ffn_gate_up_proj': _L0_ffn_in['gate_up_proj'], 'L0_ffn_down_proj': _L0_ffn_in['down_proj'], 'L1_attn_slope_rate': _L1_attn_in['slope_rate'], 'L1_attn_Wqkv': _L1_attn_in['Wqkv'], 'L1_attn_Wg': _L1_attn_in['Wg'], 'L1_attn_norm_w': _L1_attn_in['norm_w'], 'L1_attn_Wo': _L1_attn_in['Wo'], 'L1_ffn_router_w': _L1_ffn_in['router_w'], 'L1_ffn_w_gate_up': _L1_ffn_in['w_gate_up'], 'L1_ffn_w_down': _L1_ffn_in['w_down'], 'L1_ffn_shared_gate_up': _L1_ffn_in['shared_gate_up'], 'L1_ffn_shared_down': _L1_ffn_in['shared_down']}
    _x0 = _d['L0_attn_x']
    _d['L0_attn_x'] = jax.random.normal(jax.random.fold_in(jax.random.key(seed), 1), (4, 512, 256), dtype=_x0.dtype)
    del _x0
    return _d

def reference(L0_attn_x, L0_attn_Wq, L0_attn_bq, L0_attn_Wkv, L0_attn_bkv, L0_attn_Wo, L0_attn_bo, L0_ffn_router_weight, L0_ffn_gate_up_proj, L0_ffn_down_proj, L1_attn_slope_rate, L1_attn_Wqkv, L1_attn_Wg, L1_attn_norm_w, L1_attn_Wo, L1_ffn_router_w, L1_ffn_w_gate_up, L1_ffn_w_down, L1_ffn_shared_gate_up, L1_ffn_shared_down):

    def _L0_attn_ref(x, Wq, bq, Wkv, bkv, Wo, bo):
        import jax, jax.numpy as jnp
        import numpy as np
        N_HEADS = 16
        N_KV_HEADS = 4
        WINDOW = 64
        N_META = 16
        ROPE_BASE = 10000.0

        def rotate_half(x):
            x1 = x[..., 0::2]
            x2 = x[..., 1::2]
            return jnp.stack((-x2, x1), axis=-1).reshape(x.shape)

        def apply_rope(x, positions):
            d = x.shape[-1]
            inv_freq = 1.0 / ROPE_BASE ** (jnp.arange(0, d, 2, dtype=jnp.float32) / d)
            angles = positions.astype(jnp.float32)[:, None] * inv_freq
            cos = jnp.repeat(jnp.cos(angles), 2, axis=-1)[None, None]
            sin = jnp.repeat(jnp.sin(angles), 2, axis=-1)[None, None]
            return x * cos + rotate_half(x) * sin
        B, S, E = x.shape
        hd = E // N_HEADS
        q = (x @ Wq + bq).reshape(B, S, N_HEADS, hd).transpose(0, 2, 1, 3)
        kv = (x @ Wkv + bkv).reshape(B, S, 2, N_KV_HEADS, hd)
        k = kv[:, :, 0].transpose(0, 2, 1, 3)
        v = kv[:, :, 1].transpose(0, 2, 1, 3)
        pos = jnp.arange(S)
        q = apply_rope(q, pos)
        k = apply_rope(k, pos)
        rep = N_HEADS // N_KV_HEADS
        k = jnp.repeat(k, rep, axis=1)
        v = jnp.repeat(v, rep, axis=1)
        meta_end = min(N_META, S)
        scale = 1.0 / float(np.sqrt(hd))
        chunks = []
        for qs in range(0, S, WINDOW):
            qe = min(qs + WINDOW, S)
            ls = max(meta_end, qs - WINDOW + 1)
            q_c = q[:, :, qs:qe]
            k_c = jnp.concatenate([k[:, :, :meta_end], k[:, :, ls:qe]], axis=2)
            v_c = jnp.concatenate([v[:, :, :meta_end], v[:, :, ls:qe]], axis=2)
            k_pos = jnp.concatenate([jnp.arange(meta_end), jnp.arange(ls, qe)])
            q_pos = jnp.arange(qs, qe)
            causal = k_pos[None, :] <= q_pos[:, None]
            in_window = k_pos[None, :] >= q_pos[:, None] - WINDOW + 1
            meta = k_pos[None, :] < meta_end
            allowed = causal & (in_window | meta)
            scores = jnp.einsum('bhqd,bhkd->bhqk', q_c, k_c) * scale
            scores = jnp.where(allowed[None, None], scores, -jnp.inf)
            attn = jax.nn.softmax(scores, axis=-1)
            chunks.append(jnp.einsum('bhqk,bhkd->bhqd', attn, v_c))
        y = jnp.concatenate(chunks, axis=2)
        y = y.transpose(0, 2, 1, 3).reshape(B, S, E)
        return y @ Wo + bo

    def _L0_ffn_ref(hidden_states, router_weight, gate_up_proj, down_proj):
        import jax, jax.numpy as jnp
        import numpy as np
        TOP_K = 8
        CAPACITY = 128
        B, S, H = hidden_states.shape
        E = router_weight.shape[0]
        K, C = (TOP_K, CAPACITY)
        x = hidden_states.reshape(-1, H)
        logits = x @ router_weight.T
        probs = jax.nn.softmax(logits, axis=-1)
        topw, topi = jax.lax.top_k(probs, K)
        topw = topw / jnp.sum(topw, axis=-1, keepdims=True)
        flat_e = topi.reshape(-1)
        oh = jax.nn.one_hot(flat_e, E, dtype=jnp.int32)
        pos = jnp.take_along_axis(jnp.cumsum(oh, axis=0), flat_e[:, None], axis=1)[:, 0] - 1
        x_rep = jnp.repeat(x, K, axis=0)
        xe = jnp.zeros((E, C, H), x.dtype).at[flat_e, pos].set(x_rep, mode='drop')
        gu = jnp.einsum('ech,ehf->ecf', xe, gate_up_proj)
        g, u = jnp.split(gu, 2, axis=-1)
        h = jax.nn.silu(g) * u
        ye = jnp.einsum('eci,eih->ech', h, down_proj)
        valid = pos < C
        y_flat = jnp.where(valid[:, None], ye[flat_e, jnp.minimum(pos, C - 1)], 0.0)
        y = jnp.sum(y_flat.reshape(-1, K, H) * topw.reshape(-1, K)[..., None], axis=1)
        return y.reshape(B, S, H)

    def _L1_attn_ref(x, slope_rate, Wqkv, Wg, norm_w, Wo):
        import jax, jax.numpy as jnp
        import numpy as np
        BLOCK = 32
        b, n, hid = x.shape
        h = slope_rate.shape[0]
        d = Wqkv.shape[0] // (3 * h)
        nb = n // BLOCK
        qkv = jax.nn.silu(x @ Wqkv.T).reshape(b, n, h, 3 * d)
        q, k, v = jnp.split(qkv, 3, axis=-1)
        q = q.transpose(0, 2, 1, 3)
        k = k.transpose(0, 2, 1, 3)
        v = v.transpose(0, 2, 1, 3)
        s = slope_rate.astype(jnp.float32)
        arr = jnp.arange(1, BLOCK + 1, dtype=jnp.float32)
        q_decay = jnp.exp(-s * arr[:, None])
        k_decay = jnp.exp(-s * (BLOCK - arr[:, None]))
        idx = arr[:, None] - arr[None, :]
        diag_decay = jnp.where(idx >= 0, jnp.exp(-s * idx), 0.0)
        block_decay = jnp.exp(-s * BLOCK)

        def chunk(t):
            return t.reshape(b, h, nb, BLOCK, d).transpose(2, 0, 1, 3, 4)
        qc, kc, vc = (chunk(q), chunk(k), chunk(v))

        def step(kv, qkv_blk):
            qi, ki, vi = qkv_blk
            out_nd = jnp.einsum('bhmd,bhde->bhme', qi * q_decay, kv)
            qk = jnp.einsum('bhmd,bhnd->bhmn', qi, ki) * diag_decay
            out_d = jnp.einsum('bhmn,bhne->bhme', qk, vi)
            kv_new = block_decay * kv + jnp.einsum('bhmd,bhme->bhde', ki * k_decay, vi)
            return (kv_new, out_nd + out_d)
        kv0 = jnp.zeros((b, h, d, d), dtype=jnp.float32)
        _, out_blocks = jax.lax.scan(step, kv0, (qc, kc, vc))
        out = out_blocks.transpose(1, 2, 0, 3, 4).reshape(b, h, n, d)
        out = out.transpose(0, 2, 1, 3).reshape(b, n, h * d)
        eps = jnp.finfo(jnp.float32).eps
        rms = jax.lax.rsqrt(jnp.mean(out * out, axis=-1, keepdims=True) + eps)
        out = out * rms * norm_w
        gate = jax.nn.sigmoid(x @ Wg.T)
        return gate * out @ Wo.T

    def _L1_ffn_ref(hidden_states, router_w, w_gate_up, w_down, shared_gate_up, shared_down):
        import jax, jax.numpy as jnp
        import numpy as np
        B, S, D, F, E, K = (2, 256, 256, 512, 8, 1)

        def _silu_mul(gu):
            g, u = jnp.split(gu, 2, axis=-1)
            return jax.nn.silu(g) * u

        def _moe_forward(hidden_states, router_w, w_gate_up, w_down, shared_gate_up, shared_down, top_k=K):
            b, s, d = hidden_states.shape
            x = hidden_states.reshape(-1, d)
            router_logits = x @ router_w.T
            topk_vals, topk_ids = jax.lax.top_k(router_logits, top_k)
            gate = jax.nn.sigmoid(topk_vals.astype(jnp.float32)).astype(x.dtype)
            xs = (x[:, None, :] * gate[:, :, None]).reshape(-1, d)
            ids_flat = topk_ids.reshape(-1)
            n_experts = w_gate_up.shape[0]

            def body(acc, inp):
                wg, wd, e = inp
                h = _silu_mul(xs @ wg)
                o = h @ wd
                mask = (ids_flat == e)[:, None]
                return (acc + jnp.where(mask, o, jnp.zeros((), o.dtype)), None)
            acc0 = jnp.zeros_like(xs)
            routed, _ = jax.lax.scan(body, acc0, (w_gate_up, w_down, jnp.arange(n_experts)))
            routed = routed.reshape(-1, top_k, d).sum(1)
            shared = _silu_mul(x @ shared_gate_up) @ shared_down
            return (routed + shared).reshape(b, s, d)
        return _moe_forward(hidden_states, router_w, w_gate_up, w_down, shared_gate_up, shared_down)
    x = L0_attn_x
    xn = _layernorm(x, axis=-1)
    x = x + _L0_attn_ref(xn, L0_attn_Wq, L0_attn_bq, L0_attn_Wkv, L0_attn_bkv, L0_attn_Wo, L0_attn_bo) + _L0_ffn_ref(xn, L0_ffn_router_weight, L0_ffn_gate_up_proj, L0_ffn_down_proj)
    xn = _layernorm(x, axis=-1)
    x = x + _L1_attn_ref(xn, L1_attn_slope_rate, L1_attn_Wqkv, L1_attn_Wg, L1_attn_norm_w, L1_attn_Wo) + _L1_ffn_ref(xn, L1_ffn_router_w, L1_ffn_w_gate_up, L1_ffn_w_down, L1_ffn_shared_gate_up, L1_ffn_shared_down)
    return x

_drawn_inputs = setup_inputs


def setup_inputs(seed=0):
    import zlib

    import numpy as np

    out = dict(_drawn_inputs(seed))
    spreads = {'L0_attn_bq': (0.0, 0.387),
     'L0_attn_bkv': (0.0, 0.1),
     'L0_attn_bo': (0.0, 0.1),
     'L1_attn_norm_w': (1.0, 0.6)}
    factors = {'L0_ffn_router_weight': 8.0,
     'L0_ffn_gate_up_proj': 8.0,
     'L0_ffn_down_proj': 8.0,
     'L1_ffn_router_w': 7.394,
     'L1_ffn_w_gate_up': 6.995,
     'L1_ffn_w_down': 6.986,
     'L1_ffn_shared_gate_up': 2.709,
     'L1_ffn_shared_down': 2.71,
     'L1_attn_Wg': 7.621}
    for name, (base, spread) in spreads.items():
        noise = np.random.default_rng([zlib.crc32(name.encode()), seed]).standard_normal(out[name].shape)
        drawn = base * np.exp(spread * noise) if base else spread * noise
        out[name] = jnp.asarray(drawn.astype(out[name].dtype))
    for name, factor in factors.items():
        out[name] = (out[name] * factor).astype(out[name].dtype)
    return out
```

```python
from contextlib import ExitStack

import numpy as np
import concourse.bass as bass
from concourse import mybir

F32 = mybir.dt.float32
BF16 = mybir.dt.bfloat16
U32 = mybir.dt.uint32
I32 = mybir.dt.int32
ALU = mybir.AluOpType
ACT = mybir.ActivationFunctionType
AX_X = mybir.AxisListType.X

P = 128
BATCH, SEQ, D = 4, 512, 256
TOK = BATCH * SEQ
NT = TOK // P
TPB = SEQ // P
KD = D // P
LN_EPS = 1e-5

H0, G0, HD = 16, 4, 16
R0 = H0 // G0
WINDOW, N_META = 64, 16
QK = (H0 + G0) * HD
QKV = QK + G0 * HD
MASKED = -1.0e30

E0, TOPK, CAP, I0 = 64, 8, 128, 96
PROJ = QKV + E0
XROW = D + E0
SLOTS0 = TOK + CAP


def layer0_constants():
    half = np.arange(0, HD, 2, dtype=np.float32) / HD
    angle = np.arange(SEQ, dtype=np.float32)[:, None] * (1.0 / 10000.0 ** half)[None, :].astype(np.float32)
    cos = np.repeat(np.cos(angle), 2, axis=-1)
    sin = np.repeat(np.sin(angle), 2, axis=-1) * np.tile([-1.0, 1.0], HD // 2)
    rot = np.stack([np.tile(a, (1, H0 + G0)).reshape(TPB, P, QK) for a in (cos, sin)])
    q = np.arange(P)[:, None]
    k = np.arange(P)[None, :]
    own = (k <= q) & (k > q - WINDOW)
    first = np.concatenate([np.zeros((P, P), bool), own | ((k <= q) & (k < N_META))], 1)
    prev = (k >= N_META) & (k - P > q - WINDOW) | (k < N_META)
    later = np.concatenate([prev, own], 1)
    mask = np.stack([np.where(m, 0.0, MASKED) for m in (first, later)])
    return {
        "c_rot": rot.transpose(2, 0, 1, 3).reshape(P, 2 * TPB * QK).astype(np.float32),
        "c_mask": np.tile(mask, (1, 1, 2)).transpose(1, 0, 2).reshape(P, 2 * 4 * P).astype(np.float32),
        "c_ident": np.eye(P, dtype=np.float32),
        "c_order": (TOK - np.arange(TOK)).reshape(NT, P).T.astype(np.float32),
        "c_row": np.arange(P).reshape(P, 1).astype(np.float32),
    }


E1, F1 = 8, 512
RT1 = NT + E1
H1, DH1 = 16, 128
RMS_EPS = float(np.finfo(np.float32).eps)


def layer1_constants():
    i = np.arange(P)
    m = np.arange(SEQ)[None, :] - i[:, None]
    return {
        "c_tri": (i[:, None] <= i[None, :]).astype(np.float32),
        "c_prefer": np.tile(np.arange(E1, 0, -1), (P, 1)).astype(np.float32),
        "c_starts": np.tile(np.repeat(np.arange(RT1) * P, E1), (P, 1)).astype(np.float32),
        "c_lag": np.maximum(m, 0).astype(np.float32),
        "c_causal": (m >= 0).astype(np.float32),
    }


def head_weights(Wqkv, Wg):
    qkv = Wqkv.reshape(H1, 3, DH1, D)
    gate = Wg.reshape(H1, 1, DH1, D)
    return np.ascontiguousarray(np.concatenate([qkv, gate], 1).transpose(0, 3, 1, 2)).reshape(H1 * D, 4 * DH1)


def ready(t, ring=2, each=1):
    return (t + 1 + ring) * each


def freed(t, each=1):
    return (t + 1) * each


class Mem:

    def __init__(self, nc, stack, tag):
        self.nc, self.stack, self.tag = nc, stack, tag

    def sb(self, name, shape, dt=F32):
        return self.stack.enter_context(self.nc.sbuf_tensor(f"{self.tag}_{name}", shape, dt))

    def ps(self, name, shape, dt=F32):
        return self.stack.enter_context(self.nc.psum_tensor(f"{self.tag}_{name}", shape, dt))

    def sem(self, name):
        return self.stack.enter_context(self.nc.semaphore(f"{self.tag}_{name}"))


def normalise_stats(nc, x_sb, mean_rstd, x_loaded, x_loads, tag):
    with ExitStack() as stack:
        m = Mem(nc, stack, tag)
        stats = m.sb("stats", [P, NT, 6])
        veps = m.sb("veps", [P, NT])
        std = m.sb("std", [P, NT])
        stats_done, aggr_done, eps_done, sqrt_done, rstd_done = (
            m.sem(n) for n in ("stats_done", "aggr_done", "eps_done", "sqrt_done", "rstd_done"))
        block = stack.enter_context(nc.Block())

        @block.vector
        def _(dve):
            if x_loads:
                dve.wait_ge(x_loaded, x_loads)
            with dve.Fori(0, NT) as t:
                dve.bn_stats(stats[:, t, :], x_sb[:, t, :]).then_inc(stats_done, 1)
            dve.wait_ge(stats_done, NT)
            for t in range(NT):
                dve.bn_aggr(mean_rstd[:, t, :], stats[:, t, :]).then_inc(aggr_done, 1)
            dve.wait_ge(aggr_done, NT)
            dve.tensor_scalar(veps[:, :], mean_rstd[:, :, 1], LN_EPS, None, ALU.add).then_inc(eps_done, 1)
            dve.wait_ge(sqrt_done, 1)
            dve.reciprocal(mean_rstd[:, :, 1], std[:, :]).then_inc(rstd_done, 1)
            dve.wait_ge(rstd_done, 1)

        @block.scalar
        def _(act):
            act.wait_ge(eps_done, 1)
            act.activation(std[:, :], veps[:, :], ACT.Sqrt).then_inc(sqrt_done, 1)


def project0(nc, io, g):
    with ExitStack() as stack:
        m = Mem(nc, stack, "pj")
        w = m.sb("w", [P, KD, PROJ])
        bias = m.sb("bias", [P, QKV])
        rot = m.sb("rot", [P, 2, TPB, QK])
        xn = [m.sb(f"xn{s}", [P, D]) for s in range(2)]
        xnT = [m.sb(f"xnT{s}", [P, KD, P]) for s in range(2)]
        qkv = [m.sb(f"qkv{s}", [P, QKV]) for s in range(2)]
        cosx = [m.sb(f"cosx{s}", [P, QK]) for s in range(2)]
        sinx = [m.sb(f"sinx{s}", [P, QK]) for s in range(2)]
        qpad = [m.sb(f"qpad{s}", [P, R0, G0, 32]) for s in range(2)]
        kpad = [m.sb(f"kpad{s}", [P, G0, 32]) for s in range(2)]
        p_x = [m.ps(f"p_x{s}", [P, KD, P]) for s in range(2)]
        p_p = [m.ps(f"p_p{s}", [P, 512]) for s in range(2)]
        p_q = [m.ps(f"p_q{s}", [P, R0, P]) for s in range(2)]
        p_k = [m.ps(f"p_k{s}", [P, P]) for s in range(2)]
        (w_in, pads_zero, xn_ready, xT_in_psum, xT_ready, projected, qkv_ready, v_kept, cos_done,
         sin_done, pads_ready, qk_in_psum, qT_kept) = (m.sem(n) for n in (
             "w_in", "pads_zero", "xn_ready", "xT_in_psum", "xT_ready", "projected", "qkv_ready",
             "v_kept", "cos_done", "sin_done", "pads_ready", "qk_in_psum", "qT_kept"))
        xn_stored = [m.sem(f"xn_stored{s}") for s in range(2)]
        W_IN = 16 * 6
        block = stack.enter_context(nc.Block())

        @block.sync
        def _(sp):
            for s in range(2):
                sp.sem_inc(xn_stored[s], 16)
            wv = lambda a: a.rearrange("(k p) n -> p k n", p=P)
            sp.dma_start(w[:, :, 0:H0 * HD], wv(io["Wq0"])).then_inc(w_in, 16)
            sp.dma_start(w[:, :, H0 * HD:QKV], wv(io["Wkv0"])).then_inc(w_in, 16)
            sp.dma_start(w[:, :, QKV:PROJ], wv(io["routerT0"])).then_inc(w_in, 16)
            sp.dma_start(bias[:, 0:H0 * HD], io["bq0"].to_broadcast([P, H0 * HD])).then_inc(w_in, 16)
            sp.dma_start(bias[:, H0 * HD:QKV], io["bkv0"].to_broadcast([P, QKV - H0 * HD])).then_inc(w_in, 16)
            sp.dma_start(rot[:, :, :, :].rearrange("p a t n -> p (a t n)"), io["c_rot"]).then_inc(w_in, 16)
            with sp.Fori(0, NT // 2) as j:
                for s in range(2):
                    t = 2 * j + s
                    sp.wait_ge(xn_ready, ready(t))
                    sp.dma_start(g["xtab"][bass.ds(t * P, P), 0:D], xn[s][:, :]).then_inc(xn_stored[s], 16)
            for s in range(2):
                sp.wait_ge(xn_stored[s], 16 * (NT // 2 + 1))

        @block.gpsimd
        def _(pool):
            pool.sem_inc(sin_done, 4)
            for s in range(2):
                pool.memset(qpad[s][:, :, :, :], 0.0).then_inc(pads_zero, 1)
                pool.memset(kpad[s][:, :, :], 0.0).then_inc(pads_zero, 1)
            pool.wait_ge(w_in, W_IN)
            with pool.Fori(0, NT // 4) as j:
                for i in range(4):
                    t, s = 4 * j + i, i % 2
                    pool.wait_ge(qkv_ready, ready(t))
                    pool.wait_ge(pads_ready, freed(t))
                    a = qkv[s][:, 0:QK].rearrange("p (n two) -> p n two", two=2)
                    b = rot[:, 1, i, :].rearrange("p (n two) -> p n two", two=2)
                    o = sinx[s][:, :].rearrange("p (n two) -> p n two", two=2)
                    pool.tensor_tensor(o[:, :, 0], a[:, :, 1], b[:, :, 0], ALU.mult).then_inc(sin_done, 1)
                    pool.tensor_tensor(o[:, :, 1], a[:, :, 0], b[:, :, 1], ALU.mult).then_inc(sin_done, 1)

        @block.vector
        def _(dve):
            for q in (xn_ready, qkv_ready, cos_done, pads_ready):
                dve.sem_inc(q, 2)
            dve.wait_ge(w_in, W_IN)
            dve.wait_ge(pads_zero, 4)
            with dve.Fori(0, NT // 4) as j:
                for h in range(2):
                    for i in (2 * h, 2 * h + 1):
                        t, s = 4 * j + i, i % 2
                        dve.wait_ge(xT_in_psum, freed(t))
                        dve.wait_ge(xn_stored[s], freed(2 * j + h, 16))
                        dve.tensor_scalar(xn[s][:, :], g["x"][:, t, :], g["norm"][:, t, 0:1], g["norm"][:, t, 1:2],
                                          ALU.subtract, ALU.mult).then_inc(xn_ready, 1)
                    for i in (2 * h, 2 * h + 1):
                        t, s = 4 * j + i, i % 2
                        dve.wait_ge(projected, ready(t))
                        dve.wait_ge(v_kept, freed(t))
                        dve.wait_ge(sin_done, freed(t, 2))
                        dve.tensor_tensor(qkv[s][:, :], p_p[s][:, 0:QKV], bias[:, :], ALU.add).then_inc(qkv_ready, 1)
                        dve.wait_ge(qkv_ready, ready(t))
                        dve.tensor_tensor(cosx[s][:, :], qkv[s][:, 0:QK], rot[:, 0, i, :], ALU.mult).then_inc(cos_done, 1)
                        dve.wait_ge(cos_done, ready(t))
                        dve.wait_ge(sin_done, ready(t, 2, 2))
                        dve.wait_ge(qk_in_psum, freed(t))
                        nq = H0 * HD
                        v = lambda a: a[:, 0:nq].rearrange("p (g r d) -> p g r d", g=G0, r=R0)
                        dve.tensor_tensor(qpad[s][:, :, :, 0:HD].rearrange("p r g d -> p g r d"), v(cosx[s]), v(sinx[s]),
                                          ALU.add)
                        u = lambda a: a[:, nq:QK].rearrange("p (g d) -> p g d", g=G0)
                        dve.tensor_tensor(kpad[s][:, :, 0:HD], u(cosx[s]), u(sinx[s]), ALU.add).then_inc(pads_ready, 1)

        @block.scalar
        def _(act):
            for q in (xT_ready, v_kept, qT_kept):
                act.sem_inc(q, 2)
            with act.Fori(0, NT // 2) as j:
                for s in range(2):
                    t = 2 * j + s
                    act.wait_ge(xT_in_psum, ready(t))
                    act.wait_ge(projected, freed(t))
                    act.activation(xnT[s][:, :, :], p_x[s][:, :, :], ACT.Copy).then_inc(xT_ready, 1)
                for s in range(2):
                    t = 2 * j + s
                    act.wait_ge(projected, ready(t))
                    act.wait_ge(qkv_ready, ready(t))
                    act.activation(g["logits"][:, t, :], p_p[s][:, QKV:PROJ], ACT.Copy)
                    act.activation(g["V"][:, t, :], qkv[s][:, QK:QKV], ACT.Copy).then_inc(v_kept, 1)
                for s in range(2):
                    t = 2 * j + s
                    act.wait_ge(qk_in_psum, ready(t))
                    act.activation(g["qT"][:, t, :], p_q[s][:, :, :].rearrange("p r t -> p (r t)"), ACT.Copy)
                    act.activation(g["kT"][:, bass.ds(t * P, P)], p_k[s][:, :], ACT.Copy).then_inc(qT_kept, 1)
            act.wait_ge(qT_kept, NT + 2)

        @block.tensor
        def _(pe):
            for q in (xT_in_psum, projected, qk_in_psum):
                pe.sem_inc(q, 2)
            ident = g["ident"]
            pe.wait_ge(w_in, W_IN)
            with pe.Fori(0, NT // 2) as j:
                for s in range(2):
                    t = 2 * j + s
                    pe.wait_ge(xn_ready, ready(t))
                    pe.wait_ge(xT_ready, freed(t))
                    for k in range(KD):
                        mm = pe.transpose(p_x[s][:, k, :], xn[s][:, k * P:(k + 1) * P], ident[:, :])
                    mm.then_inc(xT_in_psum, 1)
                for s in range(2):
                    t = 2 * j + s
                    pe.wait_ge(xT_ready, ready(t))
                    pe.wait_ge(qkv_ready, freed(t))
                    pe.wait_ge(v_kept, freed(t))
                    for k in range(KD):
                        mm = pe.matmul(p_p[s][:, 0:PROJ], xnT[s][:, k, :], w[:, k, :], start=k == 0, stop=k == KD - 1)
                    mm.then_inc(projected, 1)
                for s in range(2):
                    t = 2 * j + s
                    pe.wait_ge(pads_ready, ready(t))
                    pe.wait_ge(qT_kept, freed(t))
                    for r in range(R0):
                        pe.transpose(p_q[s][:, r, :], qpad[s][:, r, :, :].rearrange("p g d -> p (g d)"), ident[:, :])
                    pe.transpose(p_k[s][:, :], kpad[s][:, :, :].rearrange("p g d -> p (g d)"), ident[:, :]).then_inc(qk_in_psum, 1)


def routing0(nc, io, g):
    with ExitStack() as stack:
        m = Mem(nc, stack, "rt")
        top = m.sb("top", [P, NT, 8])
        row1 = m.sb("row1", [P, NT])
        prob = m.sb("prob", [P, NT, E0])
        rest = m.sb("rest", [P, NT, E0])
        chosen = m.sb("chosen", [P, NT, E0])
        weight = m.sb("weight", [P, NT, E0])
        order = m.sb("order", [P, NT])
        row = m.sb("row", [P, 1])
        queue = m.sb("queue", [E0, TOK])
        first = m.sb("first", [E0, CAP])
        spare = m.sb("spare", [P, E0])
        lstf = m.sb("lstf", [P, E0])
        zero = m.sb("zero", [P, 17 * XROW])
        p_s = [m.ps(f"p_s{i}", [E0, 4, P]) for i in range(4)]
        p_l = m.ps("p_l", [P, E0])
        (c_in, prob_ready, chain, sel_ready, sel_in_psum, weight_ready, weight_stored, first_ready, list_in_psum,
         zeroed, tables_zero, exp_done) = (m.sem(n) for n in (
             "c_in", "prob_ready", "chain", "sel_ready", "sel_in_psum", "weight_ready", "weight_stored",
             "first_ready", "list_in_psum", "zeroed", "tables_zero", "exp_done"))
        block = stack.enter_context(nc.Block())

        @block.gpsimd
        def _(pool):
            pool.memset(zero[:, :], 0.0).then_inc(zeroed, 1)

        @block.sync
        def _(sp):
            sp.dma_start(order[:, :], io["c_order"]).then_inc(c_in, 16)
            sp.dma_start(row[:, :], io["c_row"]).then_inc(c_in, 16)
            sp.wait_ge(zeroed, 1)
            rows = SLOTS0 // P
            for a in g["acc"]:
                sp.dma_start(a.rearrange("(p n) d -> p (n d)", p=P), zero[:, 0:rows * D]).then_inc(tables_zero, 16)
            sp.dma_start(g["xtab"][TOK:SLOTS0, :], zero[:, 0:XROW]).then_inc(tables_zero, 16)
            sp.wait_ge(weight_ready, 1)
            sp.dma_start(g["xtab"][0:TOK, D:XROW].rearrange("(t p) e -> p t e", p=P), weight[:, :, :]).then_inc(weight_stored, 16)
            sp.wait_ge(tables_zero, 16 * (len(g["acc"]) + 1))
            sp.wait_ge(weight_stored, 16)

        @block.vector
        def _(dve):
            n = 0

            def step(ins):
                nonlocal n
                n += 1
                ins.then_inc(chain, 1)
                dve.wait_ge(chain, n)

            logits = g["logits"]
            step(dve.tensor_reduce(row1[:, :], logits[:, :, :], AX_X, ALU.max))
            dve.tensor_tensor(prob[:, :, :], logits[:, :, :], row1[:, :].unsqueeze(2).to_broadcast([P, NT, E0]),
                              ALU.subtract).then_inc(prob_ready, 1)
            dve.wait_ge(exp_done, 1)
            for t in range(NT):
                ins = dve.max(top[:, t, :], prob[:, t, :])
            step(ins)
            for t in range(NT):
                ins = dve.match_replace(rest[:, t, :], top[:, t, :], prob[:, t, :], -1.0)
            step(ins)
            step(dve.tensor_tensor(chosen[:, :, :], prob[:, :, :], rest[:, :, :], ALU.not_equal))
            dve.wait_ge(c_in, 32)
            dve.tensor_tensor(rest[:, :, :], chosen[:, :, :], order[:, :].unsqueeze(2).to_broadcast([P, NT, E0]),
                              ALU.mult).then_inc(sel_ready, 1)
            step(dve.tensor_tensor(weight[:, :, :], prob[:, :, :], chosen[:, :, :], ALU.mult))
            step(dve.tensor_reduce(row1[:, :], weight[:, :, :], AX_X, ALU.add))
            step(dve.reciprocal(row1[:, :], row1[:, :]))
            dve.tensor_tensor(weight[:, :, :], weight[:, :, :], row1[:, :].unsqueeze(2).to_broadcast([P, NT, E0]),
                              ALU.mult).then_inc(weight_ready, 1)
            for i in range(4):
                dve.wait_ge(sel_in_psum, i + 1)
                ins = dve.tensor_copy(queue[:, i * 4 * P:(i + 1) * 4 * P], p_s[i][:, :, :].rearrange("e a p -> e (a p)"))
            step(ins)
            for r in range(CAP // 8):
                step(dve.max(first[:, 8 * r:8 * r + 8], queue[:, :]))
                if r < CAP // 8 - 1:
                    step(dve.match_replace(queue[:, :], first[:, 8 * r:8 * r + 8], queue[:, :], -1.0))
            dve.sem_inc(first_ready, 1)
            dve.wait_ge(list_in_psum, 1)
            step(dve.tensor_scalar(spare[:, :], p_l[:, :], 0.0, row[:, 0:1], ALU.is_equal, ALU.mult))
            step(dve.scalar_tensor_tensor(lstf[:, :], p_l[:, :], -1.0, spare[:, :], ALU.mult, ALU.add))
            step(dve.tensor_scalar(g["slot_token"][:, :], lstf[:, :], float(TOK), None, ALU.add))

        @block.scalar
        def _(act):
            act.wait_ge(prob_ready, 1)
            act.activation(prob[:, :, :], prob[:, :, :], ACT.Exp).then_inc(exp_done, 1)

        @block.tensor
        def _(pe):
            ident = g["ident"]
            pe.wait_ge(sel_ready, 1)
            for t in range(NT):
                mm = pe.transpose(p_s[t // 4][:, t % 4, :], rest[:, t, :], ident[:, :])
                if t % 4 == 3:
                    mm.then_inc(sel_in_psum, 1)
            pe.wait_ge(first_ready, 1)
            pe.transpose(p_l[:, :], first[:, :], ident[0:E0, 0:E0]).then_inc(list_in_psum, 1)


def attention0(nc, io, g):
    KEYS = 2 * P
    QUADS = TPB * R0
    with ExitStack() as stack:
        m = Mem(nc, stack, "at")
        wo = m.sb("wo", [P, KD, D])
        bo = m.sb("bo", [P, D])
        maskf = m.sb("maskf", [P, 2, 2 * KEYS])
        mask = m.sb("mask", [P, 2, 2 * KEYS], BF16)
        identb = m.sb("identb", [P, P], BF16)
        qs = [m.sb(f"qs{s}", [P, R0 * P]) for s in range(2)]
        kc = [m.sb(f"kc{s}", [P, KEYS]) for s in range(2)]
        vc = [m.sb(f"vc{s}", [P, 2, G0 * HD]) for s in range(2)]
        top = [m.sb(f"top{s}", [P, G0]) for s in range(2)]
        shift = [m.sb(f"shift{s}", [P, G0]) for s in range(2)]
        pr = [m.sb(f"pr{s}", [P, G0, KEYS]) for s in range(2)]
        pT = [m.sb(f"pT{s}", [P, G0, 2, P]) for s in range(2)]
        total = [m.sb(f"total{s}", [P, H0]) for s in range(2)]
        inv = [m.sb(f"inv{s}", [P, H0]) for s in range(2)]
        y = [m.sb(f"y{s}", [P, D]) for s in range(2)]
        yT = [m.sb(f"yT{s}", [P, KD, P]) for s in range(2)]
        p_s = [m.ps(f"p_s{s}", [P, G0, KEYS]) for s in range(2)]
        p_t = [m.ps(f"p_t{s}", [P, 2, 2, P]) for s in range(2)]
        p_y = m.ps("p_y", [P, 512])
        p_o = m.ps("p_o", [P, 2, D])
        (w_in, masks_ready, base_staged, staged, scored, max_done, shift_ready, exps_done, probs_in_psum, pT_ready,
         values_done, inv_ready, y_ready, yT_in_psum, yT_ready, out_in_psum, added) = (m.sem(n) for n in (
             "w_in", "masks_ready", "base_staged", "staged", "scored", "max_done", "shift_ready", "exps_done",
             "probs_in_psum", "pT_ready", "values_done", "inv_ready", "y_ready", "yT_in_psum", "yT_ready",
             "out_in_psum", "added"))
        v_staged = m.sem("v_staged")
        block = stack.enter_context(nc.Block())
        y_step = lambda u: u >= R0 + 1 and (u - R0 - 1) % R0 == 0
        o_step = lambda u: u >= R0 + 2 and (u - R0 - 2) % R0 == 0
        STEPS = QUADS + 3

        def member(r, h):
            return 2 * (r // 2) + h // 2, 2 * (r % 2) + h % 2

        @block.sync
        def _(sp):
            sp.dma_start(wo[:, :, :], io["Wo0"].rearrange("(k p) n -> p k n", p=P)).then_inc(w_in, 16)
            sp.dma_start(bo[:, :], io["bo0"].to_broadcast([P, D])).then_inc(w_in, 16)
            sp.dma_start(maskf[:, :, :].rearrange("p a n -> p (a n)"), io["c_mask"]).then_inc(w_in, 16)
            sp.wait_ge(w_in, 48)

        @block.gpsimd
        def _(pool):
            pool.sem_inc(staged, 2)
            for s in range(2):
                pool.memset(vc[s][:, 0, :], 0.0).then_inc(base_staged, 1)
            pool.wait_ge(w_in, 48)
            with pool.Fori(0, BATCH) as b:
                for i in range(TPB):
                    t, s = TPB * b + i, i % 2
                    before = t - 1 if i else t
                    pool.wait_ge(y_ready, freed(t))
                    pool.tensor_tensor(g["x"][:, t, :], g["x"][:, t, :], bo[:, :], ALU.add)
                    pool.tensor_copy(kc[s][:, 0:N_META], g["kT"][:, bass.ds(TPB * b * P, N_META)])
                    pool.tensor_copy(kc[s][:, N_META:P], g["kT"][:, bass.ds(before * P + N_META, P - N_META)])
                    pool.tensor_copy(kc[s][:, P:KEYS], g["kT"][:, bass.ds(t * P, P)])
                    pool.tensor_copy(vc[s][:, 1, :], g["V"][:, t, :])
                    pool.tensor_copy(qs[s][:, :], g["qT"][:, t, :]).then_inc(staged, 1)

        @block.tensor
        def _(pe):
            for q in (scored, probs_in_psum, values_done, yT_in_psum, out_in_psum):
                pe.sem_inc(q, 2)
            pe.wait_ge(w_in, 48)
            pe.wait_ge(masks_ready, 2)

            def score(b, u):
                i, r, s = u // R0, u % R0, u % 2
                t, n = TPB * b + i, QUADS * b + u
                if r == 0:
                    pe.wait_ge(staged, ready(t))
                pe.wait_ge(exps_done, freed(n))
                pe.wait_ge(max_done, freed(n))
                flat = p_s[s][:, :, :].rearrange("p g k -> p (g k)")
                for half in range(2):
                    pe.matmul(flat[:, half * 512:(half + 1) * 512], identb[:, :], mask[:, min(i, 1), :],
                              start=True, stop=False, skip_group_check=True)
                for h in (0, 2, 1, 3):
                    kv, c = member(r, h)
                    mm = pe.matmul(p_s[s][:, h, :], qs[i % 2][32 * kv:32 * kv + HD, c * P:(c + 1) * P],
                                   kc[i % 2][32 * kv:32 * kv + HD, :], start=False, stop=True, skip_group_check=True)
                mm.then_inc(scored, 1)

            def values(b, u):
                i, r, s = u // R0, u % R0, u % 2
                t, n = TPB * b + i, QUADS * b + u
                pe.wait_ge(exps_done, ready(n))
                for half in range(2):
                    pe.wait_ge(pT_ready, freed(2 * n + half))
                    for h in range(2):
                        for c in range(2):
                            mm = pe.transpose(p_t[half][:, h, c, :], pr[s][:, 2 * half + h, c * P:(c + 1) * P],
                                              g["ident"][:, :])
                    mm.then_inc(probs_in_psum, 1)
                if r == 0:
                    pe.wait_ge(v_staged, ready(t))
                    pe.wait_ge(y_ready, ready(t - 1))
                for half in range(2):
                    pe.wait_ge(pT_ready, ready(2 * n + half))
                    for h in range(2 * half, 2 * half + 2):
                        kv, rep = member(r, h)
                        col = (kv * R0 + rep) * HD
                        for c in range(2):
                            mm = pe.matmul(p_y[:, col:col + HD], pT[s][:, h, c, :], vc[i % 2][:, c, kv * HD:(kv + 1) * HD],
                                           start=c == 0, stop=c == 1)
                mm.then_inc(values_done, 1)

            def turn(b, i):
                t, s = TPB * b + i, i % 2
                pe.wait_ge(y_ready, ready(t))
                pe.wait_ge(added, freed(t + 1))
                for k in range(KD):
                    mm = pe.transpose(p_o[:, 0, k * P:(k + 1) * P], y[s][:, k * P:(k + 1) * P], g["ident"][:, :])
                mm.then_inc(yT_in_psum, 1)

            def project(b, i):
                t, s = TPB * b + i, i % 2
                pe.wait_ge(yT_ready, ready(t))
                for k in range(KD):
                    mm = pe.matmul(p_o[:, 1, :], yT[s][:, k, :], wo[:, k, :], start=k == 0, stop=k == KD - 1)
                mm.then_inc(out_in_psum, 1)

            with pe.Fori(0, BATCH) as b:
                for u in range(STEPS):
                    if u < QUADS:
                        score(b, u)
                    if 1 <= u <= QUADS:
                        values(b, u - 1)
                    if y_step(u):
                        turn(b, (u - R0 - 1) // R0)
                    if o_step(u):
                        project(b, (u - R0 - 2) // R0)

        @block.scalar
        def _(act):
            for q in (exps_done, yT_ready):
                act.sem_inc(q, 2)
            with act.Fori(0, BATCH) as b:
                for u in range(STEPS):
                    if u < QUADS:
                        i, r, s = u // R0, u % R0, u % 2
                        t, n = TPB * b + i, QUADS * b + u
                        if r == 0:
                            act.wait_ge(y_ready, freed(t))
                        act.wait_ge(shift_ready, ready(n))
                        act.wait_ge(probs_in_psum, freed(n, 2))
                        for h in range(G0):
                            kv, rep = member(r, h)
                            head = kv * R0 + rep
                            ins = act.activation(pr[s][:, h, :], p_s[s][:, h, :], ACT.Exp, bias=shift[s][:, h:h + 1],
                                                 scale=HD ** -0.5, accum_out=total[i % 2][:, head:head + 1])
                        ins.then_inc(exps_done, 1)
                    if y_step(u):
                        i = (u - R0 - 1) // R0
                        t = TPB * b + i
                        act.wait_ge(yT_in_psum, ready(t))
                        act.wait_ge(out_in_psum, freed(t))
                        act.activation(yT[i % 2][:, :, :].rearrange("p k n -> p (k n)"), p_o[:, 0, :], ACT.Copy)\
                            .then_inc(yT_ready, 1)

        @block.vector
        def _(dve):
            for q in (max_done, shift_ready, inv_ready, y_ready, added, pT_ready, v_staged):
                dve.sem_inc(q, 2)
            dve.wait_ge(w_in, 48)
            dve.tensor_copy(mask[:, :, :], maskf[:, :, :]).then_inc(masks_ready, 1)
            dve.tensor_copy(identb[:, :], g["ident"][:, :]).then_inc(masks_ready, 1)
            dve.wait_ge(base_staged, 2)
            with dve.Fori(0, BATCH) as b:
                for u in range(STEPS):
                    if u % R0 == 0 and u < QUADS:
                        i = u // R0
                        before = TPB * b + max(i - 1, 0)
                        dve.tensor_copy(vc[i % 2][0:N_META, 0, :], g["V"][0:N_META, TPB * b, :])
                        dve.tensor_copy(vc[i % 2][32:64, 0, :], g["V"][32:64, before, :])
                        dve.tensor_copy(vc[i % 2][64:P, 0, :], g["V"][64:P, before, :]).then_inc(v_staged, 1)
                    if u < QUADS:
                        s, n = u % 2, QUADS * b + u
                        dve.wait_ge(scored, ready(n))
                        dve.wait_ge(exps_done, freed(n))
                        dve.tensor_reduce(top[s][:, :], p_s[s][:, :, :], AX_X, ALU.max).then_inc(max_done, 1)
                        dve.wait_ge(max_done, ready(n))
                        dve.tensor_scalar(shift[s][:, :], top[s][:, :], -(HD ** -0.5), None, ALU.mult).then_inc(shift_ready, 1)
                    if y_step(u):
                        i = (u - R0 - 1) // R0
                        t = TPB * b + i
                        dve.wait_ge(exps_done, ready(QUADS * b + R0 * i + R0 - 1))
                        dve.reciprocal(inv[i % 2][:, :], total[i % 2][:, :]).then_inc(inv_ready, 1)
                        dve.wait_ge(inv_ready, ready(t))
                        dve.wait_ge(values_done, ready(QUADS * b + R0 * i + R0 - 1))
                        dve.wait_ge(yT_in_psum, freed(t))
                        hd = lambda a: a.rearrange("p (h d) -> p h d", d=HD)
                        dve.tensor_tensor(hd(y[i % 2][:, :]), hd(p_y[:, 0:D]),
                                          inv[i % 2][:, :].unsqueeze(2).to_broadcast([P, H0, HD]), ALU.mult).then_inc(y_ready, 1)
                    if 1 <= u <= QUADS:
                        s, n = (u - 1) % 2, QUADS * b + u - 1
                        dve.wait_ge(values_done, freed(n))
                        for half in range(2):
                            dve.wait_ge(probs_in_psum, ready(2 * n + half))
                            dve.tensor_copy(pT[s][:, 2 * half:2 * half + 2, :, :], p_t[half][:, :, :, :]).then_inc(pT_ready, 1)
                    if o_step(u):
                        i = (u - R0 - 2) // R0
                        t = TPB * b + i
                        dve.wait_ge(out_in_psum, ready(t))
                        dve.wait_ge(staged, ready(t))
                        dve.tensor_tensor(g["x"][:, t, :], g["x"][:, t, :], p_o[:, 1, :], ALU.add).then_inc(added, 1)
            dve.wait_ge(added, NT + 2)


def experts0(nc, io, g):
    U = 4
    EW = 2 * I0
    with ExitStack() as stack:
        m = Mem(nc, stack, "e0")
        up = [m.sb(f"up{s}", [P, KD, EW]) for s in range(U)]
        down = [m.sb(f"down{s}", [I0, D]) for s in range(U)]
        xe = [m.sb(f"xe{s}", [P, XROW]) for s in range(U)]
        wgt = [m.sb(f"wgt{s}", [P, 1]) for s in range(U)]
        xT = [m.sb(f"xT{s}", [P, KD, P]) for s in range(2)]
        gate = [m.sb(f"gate{s}", [I0, P]) for s in range(2)]
        hT = [m.sb(f"hT{s}", [I0, P]) for s in range(2)]
        ye = [m.sb(f"ye{s}", [P, D]) for s in range(U)]
        p_x = [m.ps(f"p_x{s}", [P, KD, P]) for s in range(2)]
        p_h = [m.ps(f"p_h{s}", [I0, 2, P]) for s in range(2)]
        p_y = [m.ps(f"p_y{s}", [P, D]) for s in range(2)]
        (x_in_psum, xT_ready, h_in_psum, gate_ready, hT_ready, y_in_psum, wgt_ready,
         ye_ready) = (m.sem(n) for n in (
             "x_in_psum", "xT_ready", "h_in_psum", "gate_ready", "hT_ready",
             "y_in_psum", "wgt_ready", "ye_ready"))
        weights_in = [m.sem(f"weights_in{s}") for s in range(U)]
        gathered = [m.sem(f"gathered{s}") for s in range(U)]
        summed = [m.sem(f"summed{s}") for s in range(U)]
        block = stack.enter_context(nc.Block())

        @block.sync
        def _(sp):
            with sp.Fori(0, E0 // U) as j:
                for s in range(U):
                    e = U * j + s
                    sp.wait_ge(y_in_psum, freed(e))
                    sp.dma_start(up[s][:, :, :], io["gate_up0"][bass.ds(e, 1), :, :].rearrange("a (k p) n -> p (a k) n", p=P))\
                        .then_inc(weights_in[s], 16)
                    sp.dma_start(down[s][:, :], io["down0"][bass.ds(e, 1), :, :].rearrange("a i n -> (a i) n"))\
                        .then_inc(weights_in[s], 16)

        @block.gpsimd
        def _(pool):
            def rows(e):
                return bass.IndirectOffsetOnAxis(g["slot_token"][:, e:e + 1], 0)

            def gather(e):
                s = e % U
                if e >= U:
                    pool.wait_ge(ye_ready, freed(e))
                pool.indirect_dma_start(xe[s][:, :], None, g["xtab"][:, :], rows(e)).then_inc(gathered[s], 16)

            def scatter(e):
                s = e % U
                pool.wait_ge(ye_ready, ready(e, U))
                if e >= 2:
                    pool.wait_ge(summed[(e - 2) % U], 16 * ((e - 2) // U + 1))
                pool.indirect_dma_start(g["acc"][e % 2][:, :], rows(e), ye[s][:, :], None,
                                        compute_op=ALU.add).then_inc(summed[s], 16)

            for e in range(U):
                gather(e)
            for e in range(E0):
                scatter(e)
                if e + U < E0:
                    gather(e + U)
            for s in range(U):
                pool.wait_ge(summed[s], 16 * (E0 // U))

        @block.tensor
        def _(pe):
            for q in (x_in_psum, h_in_psum):
                pe.sem_inc(q, 2)
            pe.sem_inc(y_in_psum, U)
            ident = g["ident"]
            with pe.Fori(0, E0 // U) as j:
                def turn(s):
                    e = U * j + s
                    pe.wait_ge(gathered[s], 16 * (j + 1))
                    pe.wait_ge(xT_ready, freed(e))
                    for k in range(KD):
                        mm = pe.transpose(p_x[s % 2][:, k, :], xe[s][:, k * P:(k + 1) * P], ident[:, :])
                    mm.then_inc(x_in_psum, 1)

                def hidden(s):
                    e = U * j + s
                    pe.wait_ge(weights_in[s], 32 * (j + 1))
                    pe.wait_ge(xT_ready, ready(e))
                    pe.wait_ge(hT_ready, freed(e))
                    for half in range(2):
                        for k in range(KD):
                            mm = pe.matmul(p_h[s % 2][:, half, :], up[s][:, k, half * I0:(half + 1) * I0],
                                           xT[s % 2][:, k, :], start=k == 0, stop=k == KD - 1)
                    mm.then_inc(h_in_psum, 1)

                def output(s):
                    e = U * j + s
                    pe.wait_ge(hT_ready, ready(e))
                    pe.wait_ge(ye_ready, freed(e + 2))
                    pe.matmul(p_y[s % 2][:, :], hT[s % 2][:, :], down[s][:, :], start=True, stop=True).then_inc(y_in_psum, 1)

                for step in range(U + 2):
                    if step < U:
                        turn(step)
                    if 1 <= step <= U:
                        hidden(step - 1)
                    if step >= 2:
                        output(step - 2)

        @block.scalar
        def _(act):
            act.sem_inc(gate_ready, 2)
            act.sem_inc(ye_ready, U)

            def turn(j, first=False):
                for step in range(U + 1):
                    if step < U:
                        s, e = step, U * j + step
                        act.wait_ge(h_in_psum, ready(e))
                        act.wait_ge(hT_ready, freed(e))
                        act.activation(gate[s % 2][:, :], p_h[s % 2][:, 0, :], ACT.Silu).then_inc(gate_ready, 1)
                    if step >= 1:
                        s, e = step - 1, U * j + step - 1
                        act.wait_ge(y_in_psum, ready(e, U))
                        act.wait_ge(wgt_ready, ready(e, U))
                        if not first:
                            act.wait_ge(summed[s], 16 * j)
                        act.activation(ye[s][:, :], p_y[s % 2][:, :], ACT.Copy, scale=wgt[s][:, :]).then_inc(ye_ready, 1)

            turn(0, first=True)
            with act.Fori(1, E0 // U) as j:
                turn(j)

        @block.vector
        def _(dve):
            for q in (xT_ready, hT_ready):
                dve.sem_inc(q, 2)
            dve.sem_inc(wgt_ready, U)
            with dve.Fori(0, E0 // U) as j:
                for step in range(U + 1):
                    if step < U:
                        s, e = step, U * j + step
                        dve.wait_ge(x_in_psum, ready(e))
                        dve.wait_ge(h_in_psum, freed(e))
                        dve.tensor_copy(xT[s % 2][:, :, :], p_x[s % 2][:, :, :]).then_inc(xT_ready, 1)
                        dve.wait_ge(ye_ready, freed(e))
                        dve.tensor_copy(wgt[s][:, :], xe[s][:, bass.ds(D + e, 1)]).then_inc(wgt_ready, 1)
                    if step >= 1:
                        s, e = step - 1, U * j + step - 1
                        dve.wait_ge(gate_ready, ready(e))
                        dve.wait_ge(y_in_psum, freed(e + 2))
                        dve.tensor_tensor(hT[s % 2][:, :], gate[s % 2][:, :], p_h[s % 2][:, 1, :], ALU.mult).then_inc(hT_ready, 1)


def combine0(nc, g):
    with ExitStack() as stack:
        m = Mem(nc, stack, "cb")
        part = [m.sb(f"part{i}", [P, NT, D]) for i in range(2)]
        part_in = [m.sem(f"part_in{i}") for i in range(2)]
        added = m.sem("added")
        block = stack.enter_context(nc.Block())

        @block.sync
        def _(sp):
            for i in range(2):
                sp.dma_start(part[i][:, :, :], g["acc"][i][0:TOK, :].rearrange("(t p) d -> p t d", p=P)).then_inc(part_in[i], 16)

        @block.vector
        def _(dve):
            for i in range(2):
                dve.wait_ge(part_in[i], 16)
                if i:
                    dve.wait_ge(added, 1)
                dve.tensor_tensor(g["x"][:, :, :], g["x"][:, :, :], part[i][:, :, :], ALU.add).then_inc(added, 1)
            dve.wait_ge(added, 2)


def project1(nc, io, g):
    with ExitStack() as stack:
        m = Mem(nc, stack, "p1")
        w = m.sb("w", [P, KD, E1])
        xn = [m.sb(f"xn{s}", [P, D]) for s in range(2)]
        xT = [m.sb(f"xT{s}", [P, KD, P]) for s in range(2)]
        p_x = [m.ps(f"p_x{s}", [P, KD, P]) for s in range(2)]
        p_r = [m.ps(f"p_r{s}", [P, E1]) for s in range(2)]
        w_in, xn_ready, x_in_psum, xT_ready, routed, logits_kept = (m.sem(n) for n in (
            "w_in", "xn_ready", "x_in_psum", "xT_ready", "routed", "logits_kept"))
        rows_stored = [m.sem(f"rows_stored{s}") for s in range(2)]
        cols_stored = [m.sem(f"cols_stored{s}") for s in range(2)]
        block = stack.enter_context(nc.Block())

        @block.sync
        def _(sp):
            for s in range(2):
                sp.sem_inc(rows_stored[s], 16)
                sp.sem_inc(cols_stored[s], 16)
            sp.dma_start(w[:, :, :], io["routerT1"].rearrange("(k p) n -> p k n", p=P)).then_inc(w_in, 16)
            with sp.Fori(0, NT // 2) as j:
                for s in range(2):
                    t = 2 * j + s
                    sp.wait_ge(xT_ready, ready(t))
                    sp.wait_ge(xn_ready, ready(t))
                    sp.dma_start(g["rows1"][bass.ds(RT1 * P + t * P, P), :], xn[s][:, :]).then_inc(rows_stored[s], 16)
                    sp.dma_start(g["cols1"][:, :, bass.ds(t * P, P)], xT[s][:, :, :]).then_inc(cols_stored[s], 16)
            for s in range(2):
                sp.wait_ge(rows_stored[s], 16 * (NT // 2 + 1))
                sp.wait_ge(cols_stored[s], 16 * (NT // 2 + 1))

        @block.vector
        def _(dve):
            dve.sem_inc(xn_ready, 2)
            with dve.Fori(0, NT // 2) as j:
                for s in range(2):
                    t = 2 * j + s
                    dve.wait_ge(x_in_psum, freed(t))
                    dve.wait_ge(rows_stored[s], freed(j, 16))
                    dve.tensor_scalar(xn[s][:, :], g["x"][:, t, :], g["norm"][:, t, 0:1], g["norm"][:, t, 1:2],
                                      ALU.subtract, ALU.mult).then_inc(xn_ready, 1)

        @block.scalar
        def _(act):
            act.sem_inc(xT_ready, 2)
            act.sem_inc(logits_kept, 2)
            with act.Fori(0, NT // 2) as j:
                for s in range(2):
                    t = 2 * j + s
                    act.wait_ge(x_in_psum, ready(t))
                    act.wait_ge(routed, freed(t))
                    act.wait_ge(cols_stored[s], freed(j, 16))
                    act.activation(xT[s][:, :, :], p_x[s][:, :, :], ACT.Copy).then_inc(xT_ready, 1)
                for s in range(2):
                    t = 2 * j + s
                    act.wait_ge(routed, ready(t))
                    act.activation(g["logits1"][:, t, :], p_r[s][:, :], ACT.Copy).then_inc(logits_kept, 1)
            act.wait_ge(logits_kept, NT + 2)

        @block.tensor
        def _(pe):
            pe.sem_inc(x_in_psum, 2)
            pe.sem_inc(routed, 2)
            pe.wait_ge(w_in, 16)
            with pe.Fori(0, NT // 2) as j:
                for s in range(2):
                    t = 2 * j + s
                    pe.wait_ge(xn_ready, ready(t))
                    pe.wait_ge(xT_ready, freed(t))
                    for k in range(KD):
                        mm = pe.transpose(p_x[s][:, k, :], xn[s][:, k * P:(k + 1) * P], g["ident"][:, :])
                    mm.then_inc(x_in_psum, 1)
                for s in range(2):
                    t = 2 * j + s
                    pe.wait_ge(xT_ready, ready(t))
                    pe.wait_ge(logits_kept, freed(t))
                    for k in range(KD):
                        mm = pe.matmul(p_r[s][:, :], xT[s][:, k, :], w[:, k, :], start=k == 0, stop=k == KD - 1)
                    mm.then_inc(routed, 1)


def routing1(nc, io, g):
    with ExitStack() as stack:
        m = Mem(nc, stack, "r1")
        tri = m.sb("tri", [P, P])
        ones = m.sb("ones", [P, P])
        prefer = m.sb("prefer", [P, E1])
        starts = m.sb("starts", [P, RT1, E1])
        best = m.sb("best", [P, NT])
        gate = m.sb("gate", [P, NT])
        rgate = m.sb("rgate", [P, NT])
        cand = m.sb("cand", [P, NT, E1])
        chosen = m.sb("chosen", [P, NT, E1])
        counts = m.sb("counts", [P, E1, NT])
        until = m.sb("until", [P, E1, NT])
        n_e = m.sb("n_e", [P, E1])
        n_i = m.sb("n_i", [P, E1], I32)
        room = m.sb("room", [P, E1])
        end = m.sb("end", [P, E1])
        shift = m.sb("shift", [P, E1])
        full = m.sb("full", [P, RT1, E1])
        passed = m.sb("passed", [P, RT1])
        slotf = m.sb("slotf", [P, NT])
        xs = [m.sb(f"xs{s}", [P, D]) for s in range(2)]
        row_out = [m.sb(f"row_out{s}", [P, 1], U32) for s in range(2)]
        zero = m.sb("zero", [P, RT1 * D // 2])
        p_r = m.ps("p_r", [P, NT, E1])
        p_n = m.ps("p_n", [P, NT, E1])
        c_in, chain, chosen_ready, ranked, best_ready, gate_ready, zeroed, cleared, slots_ready, xs_ready, row_ready = (
            m.sem(n) for n in ("c_in", "chain", "chosen_ready", "ranked", "best_ready", "gate_ready", "zeroed",
                               "cleared", "slots_ready", "xs_ready", "row_ready"))
        scattered = [m.sem(f"scattered{s}") for s in range(2)]
        block = stack.enter_context(nc.Block())

        @block.sync
        def _(sp):
            sp.dma_start(tri[:, :], io["c_tri"]).then_inc(c_in, 16)
            sp.dma_start(prefer[:, :], io["c_prefer"]).then_inc(c_in, 16)
            sp.dma_start(starts[:, :, :].rearrange("p t e -> p (t e)"), io["c_starts"]).then_inc(c_in, 16)
            sp.wait_ge(zeroed, 2)
            v = g["rows1"][0:RT1 * P, :].rearrange("(p n) d -> p (n d)", p=P)
            for half in range(2):
                w = RT1 * D // 2
                sp.dma_start(v[:, half * w:(half + 1) * w], zero[:, :]).then_inc(cleared, 16)
            sp.wait_ge(cleared, 32)

        @block.scalar
        def _(act):
            act.wait_ge(best_ready, 1)
            act.activation(gate[:, :], best[:, :], ACT.Sigmoid).then_inc(gate_ready, 1)

        @block.tensor
        def _(pe):
            pe.wait_ge(c_in, 48)
            pe.wait_ge(zeroed, 2)
            pe.wait_ge(chosen_ready, 1)
            flat = lambda a: a[:, :, :].rearrange("p t e -> p (t e)")
            pe.matmul(flat(p_r), tri[:, :], flat(chosen), start=True, stop=True)
            pe.matmul(flat(p_n), ones[:, :], flat(chosen), start=True, stop=True).then_inc(ranked, 1)

        @block.vector
        def _(dve):
            n = 0

            def step(ins):
                nonlocal n
                n += 1
                ins.then_inc(chain, 1)
                dve.wait_ge(chain, n)

            logits = g["logits1"]
            wide = lambda a: a[:, :].unsqueeze(2).to_broadcast([P, NT, E1])
            dve.tensor_reduce(best[:, :], logits[:, :, :], AX_X, ALU.max).then_inc(best_ready, 1)
            dve.wait_ge(best_ready, 1)
            dve.wait_ge(c_in, 48)
            step(dve.tensor_tensor(cand[:, :, :], logits[:, :, :], wide(best), ALU.is_equal))
            step(dve.tensor_tensor(cand[:, :, :], cand[:, :, :], prefer[:, :].unsqueeze(1).to_broadcast([P, NT, E1]), ALU.mult))
            step(dve.tensor_reduce(slotf[:, :], cand[:, :, :], AX_X, ALU.max))
            dve.tensor_tensor(chosen[:, :, :], cand[:, :, :], wide(slotf), ALU.is_equal).then_inc(chosen_ready, 1)
            dve.wait_ge(ranked, 1)
            step(dve.tensor_copy(counts[:, :, :], p_n[:, :, :].rearrange("p t e -> p e t")))
            flat = lambda a: a[:, :, :].rearrange("p e t -> p (e t)")
            step(dve.tensor_tensor_scan(flat(until), ones[:, :], flat(counts), 0.0, ALU.mult, ALU.add))
            step(dve.tensor_tensor(until[:, :, :], until[:, :, :], counts[:, :, :], ALU.subtract))
            step(dve.tensor_reduce(n_e[:, :], counts[:, :, :], AX_X, ALU.add))
            step(dve.tensor_scalar(n_i[:, :], n_e[:, :], float(P - 1), None, ALU.add))
            step(dve.tensor_scalar(n_i[:, :], n_i[:, :], 7, 7, ALU.arith_shift_right, ALU.arith_shift_left))
            step(dve.tensor_copy(room[:, :], n_i[:, :]))
            step(dve.tensor_tensor_scan(end[:, :], ones[:, 0:E1], room[:, :], 0.0, ALU.mult, ALU.add))
            step(dve.tensor_tensor(shift[:, :], end[:, :], room[:, :], ALU.subtract))
            step(dve.tensor_tensor(shift[:, :], shift[:, :], until[:, :, 0], ALU.subtract))
            step(dve.tensor_tensor(until[:, :, :], until[:, :, :], shift[:, :].unsqueeze(2).to_broadcast([P, E1, NT]), ALU.add))
            step(dve.tensor_tensor(cand[:, :, :], p_r[:, :, :], until[:, :, :].rearrange("p e t -> p t e"), ALU.add))
            step(dve.tensor_tensor(cand[:, :, :], cand[:, :, :], chosen[:, :, :], ALU.mult))
            step(dve.tensor_reduce(slotf[:, :], cand[:, :, :], AX_X, ALU.add))
            dve.tensor_scalar(g["slot1"][:, :], slotf[:, :], -1.0, None, ALU.add).then_inc(slots_ready, 1)
            step(dve.tensor_tensor(full[:, :, :], starts[:, :, :], end[:, :].unsqueeze(1).to_broadcast([P, RT1, E1]), ALU.is_ge))
            step(dve.tensor_reduce(passed[:, :], full[:, :, :], AX_X, ALU.add))
            step(dve.tensor_scalar(g["tile_expert"][0:1, 0:RT1], passed[0:1, :], float(E1 - 1), None, ALU.min))
            step(dve.memset(g["tile_expert"][0:1, RT1:RT1 + NT], E1))
            dve.wait_ge(gate_ready, 1)
            dve.sem_inc(xs_ready, 2)
            step(dve.tensor_tensor(rgate[:, :], gate[:, :], g["norm"][:, :, 1], ALU.mult))
            for t in range(NT):
                s = t % 2
                if t >= 2:
                    dve.wait_ge(scattered[s], 16 * (t // 2))
                dve.tensor_scalar(xs[s][:, :], g["x"][:, t, :], g["norm"][:, t, 0:1], rgate[:, t:t + 1],
                                  ALU.subtract, ALU.mult).then_inc(xs_ready, 1)

        @block.gpsimd
        def _(pool):
            pool.memset(zero[:, :], 0.0).then_inc(zeroed, 1)
            pool.memset(ones[:, :], 1.0).then_inc(zeroed, 1)
            pool.wait_ge(slots_ready, 1)
            pool.wait_ge(cleared, 32)
            for t in range(NT):
                s = t % 2
                pool.wait_ge(xs_ready, ready(t))
                pool.indirect_dma_start(g["rows1"][:, :], bass.IndirectOffsetOnAxis(g["slot1"][:, t:t + 1], 0),
                                        xs[s][:, :], None).then_inc(scattered[s], 16)
            for s in range(2):
                pool.wait_ge(scattered[s], 16 * (NT // 2))


def experts1(nc, io, g):
    HC = F1 // P
    with ExitStack() as stack:
        m = Mem(nc, stack, "e1")
        up, down = g["up1"], g["down1"]
        xe = [m.sb(f"xe{s}", [P, D]) for s in range(2)]
        xT = [m.sb(f"xT{s}", [P, KD, P]) for s in range(2)]
        gate = [m.sb(f"gate{s}", [P, F1]) for s in range(2)]
        h = [m.sb(f"h{s}", [P, F1]) for s in range(2)]
        hT = [m.sb(f"hT{s}", [P, HC, P]) for s in range(2)]
        ye = [m.sb(f"ye{s}", [P, D]) for s in range(2)]
        p_x = m.ps("p_x", [P, KD, P])
        p_g = [m.ps(f"p_g{s}", [P, F1]) for s in range(2)]
        p_u = [m.ps(f"p_u{s}", [P, F1]) for s in range(2)]
        p_h = m.ps("p_h", [P, HC, P])
        p_y = [m.ps(f"p_y{s}", [P, D]) for s in range(2)]
        x_in_psum, xT_ready, up_done, gate_ready, h_ready, h_in_psum, hT_ready, y_in_psum, ye_ready = (
            m.sem(n) for n in ("x_in_psum", "xT_ready", "up_done", "gate_ready", "h_ready", "h_in_psum", "hT_ready",
                               "y_in_psum", "ye_ready"))
        xe_in = [m.sem(f"xe_in{s}") for s in range(2)]
        ye_stored = [m.sem(f"ye_stored{s}") for s in range(2)]
        weights_in = g["weights1_in"]
        block = stack.enter_context(nc.Block())

        @block.sync
        def _(sp):
            with sp.Fori(0, (RT1 + NT) // 2) as j:
                for s in range(2):
                    t = 2 * j + s
                    sp.wait_ge(x_in_psum, freed(t))
                    sp.dma_start(xe[s][:, :], g["rows1"][bass.ds(t * P, P), :]).then_inc(xe_in[s], 16)

        @block.gpsimd
        def _(pool):
            with pool.Fori(0, (RT1 + NT) // 2) as j:
                for s in range(2):
                    t = 2 * j + s
                    pool.wait_ge(ye_ready, ready(t))
                    pool.dma_start(g["out1"][bass.ds(t * P, P), :], ye[s][:, :]).then_inc(ye_stored[s], 16)
            for s in range(2):
                pool.wait_ge(ye_stored[s], 16 * ((RT1 + NT) // 2))

        @block.tensor
        def _(pe):
            for q in (x_in_psum, up_done, h_in_psum, y_in_psum):
                pe.sem_inc(q, 2)

            def turn(t, s, j):
                pe.wait_ge(xe_in[s], 16 * (j + 1))
                pe.wait_ge(xT_ready, freed(t + 1))
                for k in range(KD):
                    mm = pe.transpose(p_x[:, k, :], xe[s][:, k * P:(k + 1) * P], g["ident"][:, :])
                mm.then_inc(x_in_psum, 1)

            def hidden(t, s):
                e = pe.value_load(g["tile_expert"][0:1, bass.ds(t, 1)], min_val=0, max_val=E1)
                pe.wait_ge(xT_ready, ready(t))
                pe.wait_ge(h_ready, freed(t))
                for half, p in enumerate((p_g, p_u)):
                    for k in range(KD):
                        mm = pe.matmul(p[s][:, :], xT[s][:, k, :], up[:, bass.ds(e, 1), k, half * F1:(half + 1) * F1]
                                       .rearrange("p a n -> p (a n)"), start=k == 0, stop=k == KD - 1)
                mm.then_inc(up_done, 1)
                return e

            def turn_hidden(t, s):
                pe.wait_ge(h_ready, ready(t))
                pe.wait_ge(hT_ready, freed(t + 1))
                for c in range(HC):
                    mm = pe.transpose(p_h[:, c, :], h[s][:, c * P:(c + 1) * P], g["ident"][:, :])
                mm.then_inc(h_in_psum, 1)

            def output(t, s, e):
                pe.wait_ge(hT_ready, ready(t))
                pe.wait_ge(ye_ready, freed(t))
                for c in range(HC):
                    mm = pe.matmul(p_y[s][:, :], hT[s][:, c, :], down[:, bass.ds(e, 1), c, :].rearrange("p a n -> p (a n)"),
                                   start=c == 0, stop=c == HC - 1)
                mm.then_inc(y_in_psum, 1)

            pe.wait_ge(weights_in, g["weights1_n"])
            with pe.Fori(0, (RT1 + NT) // 2) as j:
                a, b = 2 * j, 2 * j + 1
                turn(a, 0, j)
                turn(b, 1, j)
                ea = hidden(a, 0)
                eb = hidden(b, 1)
                turn_hidden(a, 0)
                output(a, 0, ea)
                turn_hidden(b, 1)
                output(b, 1, eb)

        @block.scalar
        def _(act):
            for q in (gate_ready, hT_ready):
                act.sem_inc(q, 2)
            with act.Fori(0, (RT1 + NT) // 2) as j:
                for s in range(2):
                    t = 2 * j + s
                    act.wait_ge(up_done, ready(t))
                    act.wait_ge(h_ready, freed(t))
                    act.activation(gate[s][:, :], p_g[s][:, :], ACT.Silu).then_inc(gate_ready, 1)
                for s in range(2):
                    t = 2 * j + s
                    act.wait_ge(h_in_psum, ready(t))
                    act.wait_ge(y_in_psum, freed(t))
                    act.activation(hT[s][:, :, :], p_h[:, :, :], ACT.Copy).then_inc(hT_ready, 1)

        @block.vector
        def _(dve):
            for q in (xT_ready, h_ready, ye_ready):
                dve.sem_inc(q, 2)

            def body(j, first=False):
                for s in range(2):
                    t = 2 * j + s
                    dve.wait_ge(x_in_psum, ready(t))
                    dve.wait_ge(up_done, freed(t))
                    dve.tensor_copy(xT[s][:, :, :], p_x[:, :, :]).then_inc(xT_ready, 1)
                for s in range(2):
                    t = 2 * j + s
                    dve.wait_ge(gate_ready, ready(t))
                    dve.wait_ge(h_in_psum, freed(t))
                    dve.tensor_tensor(h[s][:, :], gate[s][:, :], p_u[s][:, :], ALU.mult).then_inc(h_ready, 1)
                for s in range(2):
                    t = 2 * j + s
                    dve.wait_ge(y_in_psum, ready(t))
                    if not first:
                        dve.wait_ge(ye_stored[s], 16 * j)
                    dve.tensor_copy(ye[s][:, :], p_y[s][:, :]).then_inc(ye_ready, 1)

            body(0, first=True)
            with dve.Fori(1, (RT1 + NT) // 2) as j:
                body(j)


def gather1(nc, g):
    with ExitStack() as stack:
        m = Mem(nc, stack, "g1")
        routed = m.sb("routed", [P, NT, D])
        shared = m.sb("shared", [P, NT, D])
        routed_in, shared_in, added = (m.sem(n) for n in ("routed_in", "shared_in", "added"))
        block = stack.enter_context(nc.Block())

        @block.sync
        def _(sp):
            sp.dma_start(shared[:, :, :], g["out1"][RT1 * P:(RT1 + NT) * P, :].rearrange("(t p) d -> p t d", p=P)).then_inc(shared_in, 16)

        @block.gpsimd
        def _(pool):
            for t in range(NT):
                pool.indirect_dma_start(routed[:, t, :], None, g["out1"][:, :],
                                        bass.IndirectOffsetOnAxis(g["slot1"][:, t:t + 1], 0)).then_inc(routed_in, 16)

        @block.vector
        def _(dve):
            dve.wait_ge(shared_in, 16)
            dve.tensor_tensor(g["x"][:, :, :], g["x"][:, :, :], shared[:, :, :], ALU.add).then_inc(added, 1)
            dve.wait_ge(added, 1)
            dve.wait_ge(routed_in, 16 * NT)
            dve.tensor_tensor(g["x"][:, :, :], g["x"][:, :, :], routed[:, :, :], ALU.add).then_inc(added, 1)
            dve.wait_ge(added, 2)


def decay1(nc, io, g):
    with ExitStack() as stack:
        m = Mem(nc, stack, "dc")
        lag = m.sb("lag", [P, SEQ])
        causal = m.sb("causal", [P, SEQ])
        slope = m.sb("slope", [P, H1])
        rate = m.sb("rate", [P, H1])
        scale = m.sb("scale", [P, H1])
        norm = m.sb("norm", [P, H1])
        c_in, rate_ready, exp_done, masked, scale_ready, wo_ready = (m.sem(n) for n in (
            "c_in", "rate_ready", "exp_done", "masked", "scale_ready", "wo_ready"))
        block = stack.enter_context(nc.Block())

        @block.sync
        def _(sp):
            sp.dma_start(lag[:, :], io["c_lag"]).then_inc(c_in, 16)
            sp.dma_start(causal[:, :], io["c_causal"]).then_inc(c_in, 16)
            sp.dma_start(slope[:, :], io["slope1"].to_broadcast([P, H1])).then_inc(c_in, 16)
            sp.dma_start(norm[:, :], io["norm1T"]).then_inc(c_in, 16)
            sp.dma_start(g["wo1"][:, :, :], io["WoT1"].rearrange("(h p) n -> p h n", p=P)).then_inc(c_in, 16)
            sp.wait_ge(c_in, 80)

        @block.vector
        def _(dve):
            dve.wait_ge(c_in, 80)
            dve.tensor_scalar(rate[:, :], slope[:, :], -1.0, None, ALU.mult).then_inc(rate_ready, 1)
            dve.tensor_scalar(scale[:, :], norm[:, :], 0.5, None, ALU.mult).then_inc(scale_ready, 1)
            dve.wait_ge(scale_ready, 1)
            dve.tensor_tensor(g["wo1"][:, :, :], g["wo1"][:, :, :], scale[:, :].unsqueeze(2).to_broadcast([P, H1, D]),
                              ALU.mult).then_inc(wo_ready, 1)
            with dve.Fori(0, H1) as h:
                dve.wait_ge(exp_done, h + 1)
                dve.tensor_tensor(g["decay"][:, h, :], g["decay"][:, h, :], causal[:, :], ALU.mult).then_inc(masked, 1)
            dve.wait_ge(masked, H1)

        @block.scalar
        def _(act):
            act.wait_ge(rate_ready, 1)
            with act.Fori(0, H1) as h:
                act.activation(g["decay"][:, h, :], lag[:, :], ACT.Exp, scale=rate[:, bass.ds(h, 1)]).then_inc(exp_done, 1)


def attention1(nc, io, g, out):
    DB = SEQ // P
    with ExitStack() as stack:
        m = Mem(nc, stack, "a1")
        xT = m.sb("xT", [P, KD, SEQ])
        w = [m.sb(f"w{s}", [P, KD, 4 * DH1]) for s in range(2)]
        q = [m.sb(f"q{s}", [P, SEQ]) for s in range(2)]
        k = [m.sb(f"k{s}", [P, SEQ]) for s in range(2)]
        v = [m.sb(f"v{s}", [P, DB, DH1]) for s in range(2)]
        th = [m.sb(f"th{s}", [P, SEQ]) for s in range(2)]
        sc = [m.sb(f"sc{s}", [P, DB, SEQ]) for s in range(2)]
        sq = [m.sb(f"sq{s}", [P, SEQ]) for s in range(2)]
        sqsum = m.sb("sqsum", [P, SEQ])
        ones = m.sb("ones", [P, 1])
        gated = m.sb("gated", [P, H1, SEQ])
        ms = m.sb("ms", [P, DB])
        rms = m.sb("rms", [P, DB])
        y = m.sb("y", [P, DB, D])
        p_p = [m.ps(f"p_p{s}", [P, SEQ]) for s in range(2)]
        p_s = [m.ps(f"p_s{s}", [P, SEQ]) for s in range(2)]
        p_o = [m.ps(f"p_o{s}", [P, SEQ]) for s in range(2)]
        p_w = [m.ps(f"p_w{s}", [P, 2, D]) for s in range(2)]
        names = ("x_in", "projected", "activated", "scored", "decayed", "out_in_psum", "squared", "summed", "gated_ready",
                 "sum_in_psum", "mean_ready", "root_ready", "rms_ready", "rows_in_psum", "y_ready", "y_stored", "ones_ready")
        (x_in, projected, activated, scored, decayed, out_in_psum, squared, summed, gated_ready, sum_in_psum,
         mean_ready, root_ready, rms_ready, rows_in_psum, y_ready, y_stored, ones_ready) = (m.sem(n) for n in names)
        w_in = [m.sem(f"w_in{s}") for s in range(2)]
        block = stack.enter_context(nc.Block())
        HP = H1 // 2

        @block.sync
        def _(sp):
            sp.sem_inc(y_stored, 16)
            with sp.Fori(0, BATCH) as b:
                first = sp.snap(b * SEQ)
                sp.wait_ge(projected, 4 * H1 * b + 8)
                sp.dma_start(xT[:, :, :], g["cols1"][:, :, bass.ds(first, SEQ)]).then_inc(x_in, 16)
                with sp.Fori(0, HP) as j:
                    for s in range(2):
                        h = 2 * j + s
                        row = sp.snap(h * D)
                        sp.wait_ge(projected, freed(H1 * b + h, 4))
                        sp.dma_start(w[s][:, :, :], io["Wh1"][bass.ds(row, D), :].rearrange("(k p) n -> p k n", p=P))\
                            .then_inc(w_in[s], 16)
                sp.wait_ge(y_ready, b + 1)
                sp.dma_start(out[bass.ds(b * SEQ, SEQ), :].rearrange("(t p) d -> p t d", p=P), y[:, :, :]).then_inc(y_stored, 16)
            sp.wait_ge(y_stored, 16 * (BATCH + 1))

        @block.tensor
        def _(pe):
            for sem in (scored, out_in_psum):
                pe.sem_inc(sem, 2)
            pe.sem_inc(projected, 8)
            pe.wait_ge(ones_ready, 1)

            def project(b, pair, s):
                n = H1 * b + 2 * pair + s
                pe.wait_ge(w_in[s], 16 * (HP * b + pair + 1))
                for c in range(4):
                    pe.wait_ge(activated, freed(4 * n + c))
                    bank = p_p[c % 2]
                    if c == 2:
                        for t in range(DB):
                            for kk in range(KD):
                                mm = pe.matmul(bank[:, t * P:(t + 1) * P], xT[:, kk, t * P:(t + 1) * P],
                                               w[s][:, kk, c * P:(c + 1) * P], start=kk == 0, stop=kk == KD - 1)
                    else:
                        for kk in range(KD):
                            mm = pe.matmul(bank[:, :], w[s][:, kk, c * P:(c + 1) * P], xT[:, kk, :],
                                           start=kk == 0, stop=kk == KD - 1)
                    mm.then_inc(projected, 1)

            def attend(b, h, s):
                n = H1 * b + h

                def score(c):
                    if c == 0:
                        pe.wait_ge(activated, ready(4 * n + 1))
                    pe.wait_ge(decayed, freed(4 * n + c))
                    pe.matmul(p_s[c % 2][:, 0:SEQ - c * P], k[s][:, c * P:(c + 1) * P], q[s][:, c * P:SEQ],
                              start=True, stop=True).then_inc(scored, 1)

                def value(c):
                    if c == 0:
                        pe.wait_ge(activated, ready(4 * n + 2))
                        pe.wait_ge(gated_ready, freed(n))
                        pe.wait_ge(squared, freed(n))
                    pe.wait_ge(decayed, ready(4 * n + c))
                    mm = pe.matmul(p_o[s][:, c * P:SEQ], v[s][:, c, :], sc[s][:, c, 0:SEQ - c * P],
                                   start=c == 0, stop=c == DB - 1)
                    if c == DB - 1:
                        mm.then_inc(out_in_psum, 1)

                score(0)
                score(1)
                for c in range(DB):
                    value(c)
                    if c + 2 < DB:
                        score(c + 2)

            with pe.Fori(0, BATCH) as b:
                pe.wait_ge(x_in, 16 * (b + 1))
                project(b, 0, 0)
                with pe.Fori(0, HP - 1) as j:
                    project(b, j, 1)
                    attend(b, 2 * j, 0)
                    project(b, j + 1, 0)
                    attend(b, 2 * j + 1, 1)
                project(b, HP - 1, 1)
                attend(b, H1 - 2, 0)
                attend(b, H1 - 1, 1)
                pe.wait_ge(gated_ready, ready(H1 * b + H1 - 1))
                for t in range(DB):
                    for h in range(H1):
                        mm = pe.matmul(p_w[t // 2][:, t % 2, :], gated[:, h, t * P:(t + 1) * P], g["wo1"][:, h, :],
                                       start=h == 0, stop=h == H1 - 1)
                mm.then_inc(rows_in_psum, 1)
                pe.wait_ge(summed, H1 * (b + 1) + 2)
                pe.wait_ge(squared, ready(H1 * b + H1 - 1))
                for t in range(DB):
                    mm = pe.matmul(p_o[0][:, t:t + 1], sqsum[:, t * P:(t + 1) * P], ones[:, :], start=True, stop=True)
                mm.then_inc(sum_in_psum, 1)
                pe.wait_ge(rms_ready, b + 1)
                pe.wait_ge(y_ready, b + 1)

        @block.scalar
        def _(act):
            act.sem_inc(activated, 2)
            act.sem_inc(squared, 2)

            def activate(b, h, s):
                n = H1 * b + h
                for c in range(4):
                    act.wait_ge(projected, 4 * n + c + 9)
                    bank = p_p[c % 2]
                    if c == 0:
                        act.wait_ge(out_in_psum, freed(n))
                        act.wait_ge(gated_ready, freed(n))
                    dst = (q[s][:, :], k[s][:, :], v[s][:, :, :].rearrange("p t e -> p (t e)"), th[s][:, :])[c]
                    if c < 3:
                        act.activation(dst, bank[:, :], ACT.Silu).then_inc(activated, 1)
                    else:
                        act.activation(dst, bank[:, :], ACT.Tanh, scale=0.5).then_inc(activated, 1)

            def square(b, h, s):
                n = H1 * b + h
                act.wait_ge(out_in_psum, ready(n))
                act.wait_ge(summed, freed(n))
                act.activation(sq[s][:, :], p_o[s][:, :], ACT.Square).then_inc(squared, 1)

            with act.Fori(0, BATCH) as b:
                activate(b, 0, 0)
                with act.Fori(0, HP - 1) as j:
                    activate(b, 2 * j + 1, 1)
                    square(b, 2 * j, 0)
                    activate(b, 2 * j + 2, 0)
                    square(b, 2 * j + 1, 1)
                activate(b, H1 - 1, 1)
                square(b, H1 - 2, 0)
                square(b, H1 - 1, 1)
                act.wait_ge(mean_ready, b + 1)
                act.activation(rms[:, :], ms[:, :], ACT.Sqrt).then_inc(root_ready, 1)

        @block.gpsimd
        def _(pool):
            pool.memset(ones[:, :], 1.0).then_inc(ones_ready, 1)
            pool.sem_inc(summed, 2)
            with pool.Fori(0, BATCH) as b:
                pool.wait_ge(sum_in_psum, b + 1)
                pool.wait_ge(squared, ready(H1 * b + 1))
                pool.tensor_tensor(sqsum[:, :], sq[0][:, :], sq[1][:, :], ALU.add).then_inc(summed, 2)
                with pool.Fori(1, HP) as j:
                    for s in range(2):
                        n = H1 * b + 2 * j + s
                        pool.wait_ge(squared, ready(n))
                        pool.wait_ge(summed, freed(n + 1))
                        pool.tensor_tensor(sqsum[:, :], sqsum[:, :], sq[s][:, :], ALU.add).then_inc(summed, 1)

        @block.vector
        def _(dve):
            dve.sem_inc(decayed, 2)
            dve.sem_inc(gated_ready, 2)
            dve.sem_inc(sum_in_psum, 1)

            def attend(b, h, s):
                n = H1 * b + h
                for c in range(DB):
                    dve.wait_ge(scored, ready(4 * n + c))
                    if c == 0:
                        dve.wait_ge(out_in_psum, freed(n))
                    width = SEQ - c * P
                    dve.tensor_tensor(sc[s][:, c, 0:width], p_s[c % 2][:, 0:width], g["decay"][:, h, 0:width],
                                      ALU.mult).then_inc(decayed, 1)
                dve.wait_ge(out_in_psum, ready(n))
                dve.wait_ge(activated, ready(4 * n + 3))
                dve.wait_ge(squared, ready(n))
                dve.scalar_tensor_tensor(gated[:, h, :], th[s][:, :], 1.0, p_o[s][:, :], ALU.add, ALU.mult).then_inc(gated_ready, 1)

            with dve.Fori(0, BATCH) as b:
                with dve.Fori(0, HP) as j:
                    for s in range(2):
                        attend(b, 2 * j + s, s)
                dve.wait_ge(sum_in_psum, b + 2)
                dve.tensor_scalar(ms[:, :], p_o[0][:, 0:DB], 1.0 / (H1 * DH1), RMS_EPS, ALU.mult, ALU.add).then_inc(mean_ready, 1)
                dve.wait_ge(root_ready, b + 1)
                dve.reciprocal(rms[:, :], rms[:, :]).then_inc(rms_ready, 1)
                dve.wait_ge(rms_ready, b + 1)
                dve.wait_ge(rows_in_psum, b + 1)
                dve.wait_ge(y_stored, freed(b, 16))
                for t in range(DB):
                    ins = dve.scalar_tensor_tensor(y[:, t, :], p_w[t // 2][:, t % 2, :], rms[:, t:t + 1],
                                                   g["x"][:, DB * b + t, :], ALU.mult, ALU.add)
                ins.then_inc(y_ready, 1)


def program(nc, io, out, upto=99):
    dr = lambda name, shape, dt=F32: nc.dram_tensor(name, shape, dt, kind="Internal").ap()
    with ExitStack() as stack:
        m = Mem(nc, stack, "g")
        g = {
            "ident": m.sb("ident", [P, P]),
            "x": m.sb("x", [P, NT, D]),
            "norm": m.sb("norm", [P, NT, 2]),
            "xtab": dr("xtab", [SLOTS0, XROW]),
            "acc": [dr(f"acc{i}", [SLOTS0, D]) for i in range(2)],
            "rows1": dr("rows1", [(RT1 + NT) * P, D]),
            "out1": dr("out1", [(RT1 + NT) * P, D]),
            "cols1": dr("cols1", [P, KD, TOK]),
            "slot1": m.sb("slot1", [P, NT], U32),
            "tile_expert": m.sb("tile_expert", [1, RT1 + NT], I32),
            "logits1": m.sb("logits1", [P, NT, E1]),
            "slot_token": m.sb("slot_token", [P, E0], U32),
        }
        x_loaded = m.sem("x_loaded")
        with nc.Block() as block:
            @block.sync
            def _(sp):
                x_v = io["x"].rearrange("(t p) d -> p t d", p=P)
                for i in range(4):
                    sp.dma_start(g["x"][:, 4 * i:4 * i + 4, :], x_v[:, 4 * i:4 * i + 4, :]).then_inc(x_loaded, 16)
                sp.dma_start(g["ident"][:, :], io["c_ident"]).then_inc(x_loaded, 16)
                sp.wait_ge(x_loaded, 80)
        normalise_stats(nc, g["x"], g["norm"], None, 0, "n0")
        with ExitStack() as s0:
            m0 = Mem(nc, s0, "l0")
            g["qT"] = m0.sb("qT", [P, NT, R0 * P])
            g["kT"] = m0.sb("kT", [P, TOK])
            g["V"] = m0.sb("V", [P, NT, G0 * HD])
            g["logits"] = m0.sb("logits", [P, NT, E0])
            project0(nc, io, g)
            if upto >= 2:
                routing0(nc, io, g)
            if upto >= 3:
                attention0(nc, io, g)
        if upto >= 4:
            experts0(nc, io, g)
        if upto >= 5:
            combine0(nc, g)
            normalise_stats(nc, g["x"], g["norm"], None, 0, "n1")
            project1(nc, io, g)
            routing1(nc, io, g)
        if upto >= 6:
            with ExitStack() as s1:
                m1 = Mem(nc, s1, "w1")
                g["up1"] = m1.sb("up1", [P, E1 + 1, KD, 2 * F1])
                g["down1"] = m1.sb("down1", [P, E1 + 1, F1 // P, D])
                g["weights1_in"] = m1.sem("weights1_in")
                g["weights1_n"] = 16 * 2 * (E1 + 1)
                with nc.Block() as block:
                    @block.sync
                    def _(sp):
                        for e in range(E1 + 1):
                            u = io["gate_up1"][e] if e < E1 else io["shared_up1"]
                            d = io["down1"][e] if e < E1 else io["shared_down1"]
                            sp.dma_start(g["up1"][:, e, :, :], u.rearrange("(k p) n -> p k n", p=P)).then_inc(g["weights1_in"], 16)
                            sp.dma_start(g["down1"][:, e, :, :], d.rearrange("(k p) n -> p k n", p=P)).then_inc(g["weights1_in"], 16)
                experts1(nc, io, g)
            gather1(nc, g)
        if upto >= 7:
            with ExitStack() as s2:
                m2 = Mem(nc, s2, "w2")
                g["decay"] = m2.sb("decay", [P, H1, SEQ])
                g["wo1"] = m2.sb("wo1", [P, H1, D])
                decay1(nc, io, g)
                attention1(nc, io, g, out)


def layouts(inputs):
    a = {name: np.asarray(value) for name, value in inputs.items()}
    t = lambda name: np.ascontiguousarray(a[name].T)
    return {
        "x": a["L0_attn_x"].reshape(TOK, D),
        "Wq0": a["L0_attn_Wq"],
        "Wkv0": a["L0_attn_Wkv"],
        "bq0": a["L0_attn_bq"].reshape(1, -1),
        "bkv0": a["L0_attn_bkv"].reshape(1, -1),
        "Wo0": a["L0_attn_Wo"],
        "bo0": a["L0_attn_bo"].reshape(1, -1),
        "routerT0": t("L0_ffn_router_weight"),
        "gate_up0": a["L0_ffn_gate_up_proj"],
        "down0": a["L0_ffn_down_proj"],
        "slope1": a["L1_attn_slope_rate"].reshape(1, H1),
        "norm1T": np.ascontiguousarray(a["L1_attn_norm_w"].reshape(H1, DH1).T),
        "WoT1": t("L1_attn_Wo"),
        "Wh1": head_weights(a["L1_attn_Wqkv"], a["L1_attn_Wg"]),
        "routerT1": t("L1_ffn_router_w"),
        "gate_up1": a["L1_ffn_w_gate_up"],
        "down1": a["L1_ffn_w_down"],
        "shared_up1": a["L1_ffn_shared_gate_up"],
        "shared_down1": a["L1_ffn_shared_down"],
        **layer0_constants(),
        **layer1_constants(),
    }


def kernel(**inputs):
    from concourse import bacc
    from concourse.bass_utils import run_bass_kernel_spmd

    nc = bacc.Bacc("TRN2", target_bir_lowering=False, num_devices=1)
    arrays, io = {}, {}
    for name, value in layouts(inputs).items():
        arrays[f"in_{name}"] = np.ascontiguousarray(value)
        io[name] = nc.dram_tensor(f"in_{name}", value.shape, mybir.dt.from_np(value.dtype), kind="ExternalInput").ap()
    out = nc.dram_tensor("out_y", (TOK, D), F32, kind="ExternalOutput").ap()
    program(nc, io, out)
    result = run_bass_kernel_spmd(nc, [arrays], core_ids=[0])
    return result.results[0]["out_y"].reshape(BATCH, SEQ, D)
```

```python
from contextlib import ExitStack

import numpy as np
import concourse.bass as bass
from concourse import mybir

F32 = mybir.dt.float32
F32R = mybir.dt.float32r
BF16 = mybir.dt.bfloat16
U32 = mybir.dt.uint32
I32 = mybir.dt.int32
ALU = mybir.AluOpType
ACT = mybir.ActivationFunctionType
AX_X = mybir.AxisListType.X

P = 128
BATCH, SEQ, D = 4, 512, 256
TOK = BATCH * SEQ
NT = TOK // P
TPB = SEQ // P
KD = D // P
LN_EPS = 1e-5

H0, G0, HD = 16, 4, 16
R0 = H0 // G0
WINDOW, N_META = 64, 16
QK = (H0 + G0) * HD
QKV = QK + G0 * HD
MASKED = -1.0e30

E0, TOPK, CAP, I0 = 64, 8, 128, 96
PROJ = QKV + E0
XROW = D + E0
SLOTS0 = TOK + CAP


def layer0_constants():
    half = np.arange(0, HD, 2, dtype=np.float32) / HD
    angle = np.arange(SEQ, dtype=np.float32)[:, None] * (1.0 / 10000.0 ** half)[None, :].astype(np.float32)
    cos = np.repeat(np.cos(angle), 2, axis=-1)
    sin = np.repeat(np.sin(angle), 2, axis=-1) * np.tile([-1.0, 1.0], HD // 2)
    rot = np.stack([np.tile(a, (1, H0 + G0)).reshape(TPB, P, QK) for a in (cos, sin)])
    q = np.arange(P)[:, None]
    k = np.arange(P)[None, :]
    own = (k <= q) & (k > q - WINDOW)
    first = np.concatenate([np.zeros((P, P), bool), own | ((k <= q) & (k < N_META))], 1)
    prev = (k >= N_META) & (k - P > q - WINDOW) | (k < N_META)
    later = np.concatenate([prev, own], 1)
    mask = np.stack([np.where(m, 0.0, MASKED) for m in (first, later)])
    return {
        "c_rot": rot.transpose(2, 0, 1, 3).reshape(P, 2 * TPB * QK).astype(np.float32),
        "c_mask": mask.transpose(1, 0, 2).reshape(P, 2 * 2 * P).astype(np.float32),
        "c_maskT": mask.reshape(2, P, 2, P).transpose(3, 0, 2, 1).reshape(P, 2 * 2 * P).astype(np.float32),
        "c_ident": np.eye(P, dtype=np.float32),
        "c_order": (TOK - np.arange(TOK)).reshape(NT, P).T.astype(np.float32),
        "c_row": np.arange(P).reshape(P, 1).astype(np.float32),
    }


E1, F1 = 8, 512
RT1 = NT + E1
H1, DH1 = 16, 128
RMS_EPS = float(np.finfo(np.float32).eps)


def layer1_constants():
    i = np.arange(P)
    m = np.arange(SEQ)[None, :] - i[:, None]
    return {
        "c_tri": (i[:, None] <= i[None, :]).astype(np.float32),
        "c_prefer": np.tile(np.arange(E1, 0, -1), (P, 1)).astype(np.float32),
        "c_starts": np.tile(np.repeat(np.arange(RT1) * P, E1), (P, 1)).astype(np.float32),
        "c_lag": np.maximum(m, 0).astype(np.float32),
        "c_causal": (m >= 0).astype(np.float32),
    }


def head_weights(Wqkv, Wg):
    qkv = Wqkv.reshape(H1, 3, DH1, D)
    gate = Wg.reshape(H1, 1, DH1, D)
    return np.ascontiguousarray(np.concatenate([qkv, gate], 1).transpose(0, 3, 1, 2)).reshape(H1 * D, 4 * DH1)


def paired_heads(w):
    return np.ascontiguousarray(w.reshape(-1, G0 // 2, 2, R0, HD).transpose(0, 1, 3, 2, 4)).reshape(-1, H0 * HD)


def ready(t, ring=2, each=1):
    return (t + 1 + ring) * each


def freed(t, each=1):
    return (t + 1) * each


class Mem:

    def __init__(self, nc, stack, tag):
        self.nc, self.stack, self.tag = nc, stack, tag

    def sb(self, name, shape, dt=F32):
        return self.stack.enter_context(self.nc.sbuf_tensor(f"{self.tag}_{name}", shape, dt))

    def ps(self, name, shape, dt=F32):
        return self.stack.enter_context(self.nc.psum_tensor(f"{self.tag}_{name}", shape, dt))

    def sem(self, name):
        return self.stack.enter_context(self.nc.semaphore(f"{self.tag}_{name}"))


def normalise_stats(nc, x_sb, mean_rstd, x_loaded, x_loads, tag):
    with ExitStack() as stack:
        m = Mem(nc, stack, tag)
        stats = m.sb("stats", [P, NT, 6])
        veps = m.sb("veps", [P, NT])
        std = m.sb("std", [P, NT])
        steps_done, sqrt_done = (m.sem(n) for n in ("steps_done", "sqrt_done"))
        block = stack.enter_context(nc.Block())

        @block.vector
        def _(dve):
            if x_loads:
                dve.wait_ge(x_loaded, x_loads)
            with dve.Fori(0, NT) as t:
                dve.bn_stats(stats[:, t, :], x_sb[:, t, :]).then_inc(steps_done, 1)
            dve.wait_ge(steps_done, NT)
            for t in range(NT):
                dve.bn_aggr(mean_rstd[:, t, :], stats[:, t, :]).then_inc(steps_done, 1)
            dve.wait_ge(steps_done, 2 * NT)
            dve.tensor_scalar(veps[:, :], mean_rstd[:, :, 1], LN_EPS, None, ALU.add).then_inc(steps_done, 1)
            dve.wait_ge(sqrt_done, 1)
            dve.reciprocal(mean_rstd[:, :, 1], std[:, :]).then_inc(steps_done, 1)
            dve.wait_ge(steps_done, 2 * NT + 2)

        @block.scalar
        def _(act):
            act.wait_ge(steps_done, 2 * NT + 1)
            act.activation(std[:, :], veps[:, :], ACT.Sqrt).then_inc(sqrt_done, 1)


def project0(nc, io, g):
    with ExitStack() as stack:
        m = Mem(nc, stack, "pj")
        w = m.sb("w", [P, KD, PROJ])
        bias = m.sb("bias", [P, QKV])
        rot = m.sb("rot", [P, 2, TPB, QK])
        xn = [m.sb(f"xn{s}", [P, D]) for s in range(2)]
        xnT = [m.sb(f"xnT{s}", [P, KD, P]) for s in range(2)]
        qkv = [m.sb(f"qkv{s}", [P, QKV]) for s in range(2)]
        cosx = [m.sb(f"cosx{s}", [P, QK]) for s in range(2)]
        sinx = [m.sb(f"sinx{s}", [P, QK]) for s in range(2)]
        rotated = [m.sb(f"rotated{s}", [P, H0 + G0, HD]) for s in range(2)]
        parts = [m.sb(f"parts{s}", [P, H0 + G0, 4, HD], F32R) for s in range(2)]
        identr = m.sb("identr", [P, P], F32R)
        p_x = [m.ps(f"p_x{s}", [P, 4, P]) for s in range(2)]
        p_p = [m.ps(f"p_p{s}", [P, 512]) for s in range(2)]
        p_q = [m.ps(f"p_q{a}", [P, R0, P], F32R) for a in range(2)]
        p_k = [m.ps(f"p_k{s}", [P, 4, P], F32R) for s in range(2)]
        (w_in, ones_set, ident_ready, xn_ready, xT_in_psum, xT_ready, projected, qkv_ready, v_kept, cos_done,
         sin_done, rotated_ready, highs_ready, parts_ready, qk_in_psum, qT_kept) = (m.sem(n) for n in (
             "w_in", "ones_set", "ident_ready", "xn_ready", "xT_in_psum", "xT_ready", "projected", "qkv_ready",
             "v_kept", "cos_done", "sin_done", "rotated_ready", "highs_ready", "parts_ready", "qk_in_psum",
             "qT_kept"))
        xn_stored = [m.sem(f"xn_stored{s}") for s in range(2)]
        W_IN = 16 * 6
        block = stack.enter_context(nc.Block())

        @block.sync
        def _(sp):
            for s in range(2):
                sp.sem_inc(xn_stored[s], 16)
            wv = lambda a: a.rearrange("(k p) n -> p k n", p=P)
            sp.dma_start(w[:, :, 0:H0 * HD], wv(io["Wq0"])).then_inc(w_in, 16)
            sp.dma_start(w[:, :, H0 * HD:QKV], wv(io["Wkv0"])).then_inc(w_in, 16)
            sp.dma_start(w[:, :, QKV:PROJ], wv(io["routerT0"])).then_inc(w_in, 16)
            sp.dma_start(bias[:, 0:H0 * HD], io["bq0"].to_broadcast([P, H0 * HD])).then_inc(w_in, 16)
            sp.dma_start(bias[:, H0 * HD:QKV], io["bkv0"].to_broadcast([P, QKV - H0 * HD])).then_inc(w_in, 16)
            sp.dma_start(rot[:, :, :, :].rearrange("p a t n -> p (a t n)"), io["c_rot"]).then_inc(w_in, 16)
            with sp.Fori(0, NT // 2) as j:
                for s in range(2):
                    t = 2 * j + s
                    sp.wait_ge(xn_ready, ready(t))
                    sp.dma_start(g["xtab"][bass.ds(t * P, P), 0:D], xn[s][:, :]).then_inc(xn_stored[s], 16)
            for s in range(2):
                sp.wait_ge(xn_stored[s], 16 * (NT // 2 + 1))

        @block.gpsimd
        def _(pool):
            pool.sem_inc(sin_done, 4)
            pool.sem_inc(parts_ready, 2)
            pool.memset(g["V"][:, :, :, :], 1.0).then_inc(ones_set, 1)
            pool.wait_ge(w_in, W_IN)
            with pool.Fori(0, NT // 4) as j:
                for i in range(4):
                    t, s = 4 * j + i, i % 2
                    pool.wait_ge(qkv_ready, ready(t))
                    pool.wait_ge(rotated_ready, freed(t))
                    a = qkv[s][:, 0:QK].rearrange("p (n two) -> p n two", two=2)
                    b = rot[:, 1, i, :].rearrange("p (n two) -> p n two", two=2)
                    o = sinx[s][:, :].rearrange("p (n two) -> p n two", two=2)
                    pool.tensor_tensor(o[:, :, 0], a[:, :, 1], b[:, :, 0], ALU.mult).then_inc(sin_done, 1)
                    pool.tensor_tensor(o[:, :, 1], a[:, :, 0], b[:, :, 1], ALU.mult).then_inc(sin_done, 1)
                    pool.wait_ge(highs_ready, ready(t))
                    pool.wait_ge(qk_in_psum, freed(t, 2))
                    for i1 in (2, 3):
                        pool.tensor_tensor(parts[s][:, 0:H0, i1, :], rotated[s][:, 0:H0, :], parts[s][:, 0:H0, 0, :],
                                           ALU.subtract)
                    for i1 in (1, 3):
                        ins = pool.tensor_tensor(parts[s][:, H0:, i1, :], rotated[s][:, H0:, :],
                                                 parts[s][:, H0:, 0, :], ALU.subtract)
                    ins.then_inc(parts_ready, 1)

        @block.vector
        def _(dve):
            for q in (xn_ready, qkv_ready, cos_done, rotated_ready, highs_ready):
                dve.sem_inc(q, 2)
            dve.tensor_copy(identr[:, :], g["ident"][:, :]).then_inc(ident_ready, 1)
            dve.wait_ge(w_in, W_IN)
            with dve.Fori(0, NT // 4) as j:
                for h in range(2):
                    for i in (2 * h, 2 * h + 1):
                        t, s = 4 * j + i, i % 2
                        dve.wait_ge(xT_in_psum, freed(t))
                        dve.wait_ge(xn_stored[s], freed(2 * j + h, 16))
                        dve.tensor_scalar(xn[s][:, :], g["x"][:, t, :], g["norm"][:, t, 0:1], g["norm"][:, t, 1:2],
                                          ALU.subtract, ALU.mult).then_inc(xn_ready, 1)
                    for i in (2 * h, 2 * h + 1):
                        t, s = 4 * j + i, i % 2
                        dve.wait_ge(projected, ready(t))
                        dve.wait_ge(v_kept, freed(t))
                        dve.wait_ge(sin_done, freed(t, 2))
                        dve.tensor_tensor(qkv[s][:, :], p_p[s][:, 0:QKV], bias[:, :], ALU.add).then_inc(qkv_ready, 1)
                        dve.wait_ge(qkv_ready, ready(t))
                        dve.tensor_tensor(cosx[s][:, :], qkv[s][:, 0:QK], rot[:, 0, i, :], ALU.mult).then_inc(cos_done, 1)
                        dve.wait_ge(cos_done, ready(t))
                        dve.wait_ge(sin_done, ready(t, 2, 2))
                        dve.wait_ge(parts_ready, freed(t))
                        dve.tensor_tensor(rotated[s][:, :, :].rearrange("p h d -> p (h d)"), cosx[s][:, :], sinx[s][:, :],
                                          ALU.add).then_inc(rotated_ready, 1)
                        dve.wait_ge(rotated_ready, ready(t))
                        dve.wait_ge(qk_in_psum, freed(t, 2))
                        for i1 in range(2):
                            dve.tensor_copy(parts[s][:, 0:H0, i1, :], rotated[s][:, 0:H0, :])
                        for i1 in (0, 2):
                            ins = dve.tensor_copy(parts[s][:, H0:, i1, :], rotated[s][:, H0:, :])
                        ins.then_inc(highs_ready, 1)

        @block.scalar
        def _(act):
            for q in (xT_ready, v_kept):
                act.sem_inc(q, 2)
            act.sem_inc(qT_kept, 4)
            act.wait_ge(ones_set, 1)
            with act.Fori(0, NT // 2) as j:
                for s in range(2):
                    t = 2 * j + s
                    act.wait_ge(xT_in_psum, ready(t))
                    act.wait_ge(projected, freed(t))
                    act.activation(xnT[s][:, :, :], p_x[s][:, 0:KD, :], ACT.Copy).then_inc(xT_ready, 1)
                for s in range(2):
                    t = 2 * j + s
                    act.wait_ge(projected, ready(t))
                    act.wait_ge(qkv_ready, ready(t))
                    act.activation(g["logits"][:, t, :], p_p[s][:, QKV:PROJ], ACT.Copy)
                    act.activation(g["V"][:, t, :, 0:HD], qkv[s][:, QK:QKV].rearrange("p (g d) -> p g d", g=G0),
                                   ACT.Copy).then_inc(v_kept, 1)
                for s in range(2):
                    t = 2 * j + s
                    act.wait_ge(qk_in_psum, ready(2 * t, 4))
                    act.activation(g["kT"][:, :, bass.ds(t * P, P)], p_k[s][:, 0:2, :], ACT.Copy)
                    for a in range(2):
                        if a:
                            act.wait_ge(qk_in_psum, ready(2 * t + 1, 4))
                        act.activation(g["qT"][:, t, a, :], p_q[a][:, :, :].rearrange("p r t -> p (r t)"), ACT.Copy)\
                            .then_inc(qT_kept, 1)
            act.wait_ge(qT_kept, 2 * NT + 4)

        @block.tensor
        def _(pe):
            for q in (xT_in_psum, projected):
                pe.sem_inc(q, 2)
            pe.sem_inc(qk_in_psum, 4)
            ident = g["ident"]
            pe.wait_ge(w_in, W_IN)
            pe.wait_ge(ident_ready, 1)
            with pe.Fori(0, NT // 2) as j:
                for s in range(2):
                    t = 2 * j + s
                    pe.wait_ge(xn_ready, ready(t))
                    pe.wait_ge(xT_ready, freed(t))
                    for k in range(KD):
                        mm = pe.transpose(p_x[s][:, k, :], xn[s][:, k * P:(k + 1) * P], ident[:, :])
                    mm.then_inc(xT_in_psum, 1)
                for s in range(2):
                    t = 2 * j + s
                    pe.wait_ge(xT_ready, ready(t))
                    pe.wait_ge(qkv_ready, freed(t))
                    pe.wait_ge(v_kept, freed(t))
                    for k in range(KD):
                        mm = pe.matmul(p_p[s][:, 0:PROJ], xnT[s][:, k, :], w[:, k, :], start=k == 0, stop=k == KD - 1)
                    mm.then_inc(projected, 1)
                for s in range(2):
                    t = 2 * j + s
                    pe.wait_ge(parts_ready, ready(t))
                    for a in range(2):
                        pe.wait_ge(qT_kept, ready(2 * t + a - 2, 4))
                        if a == 0:
                            for c in range(2):
                                pe.transpose(p_k[s][:, c, :], parts[s][:, H0 + 2 * c:H0 + 2 * c + 2, :, :]
                                             .rearrange("p h i d -> p (h i d)"), identr[:, :])
                        for r in range(R0):
                            h = 2 * (R0 * a + r)
                            mm = pe.transpose(p_q[a][:, r, :], parts[s][:, h:h + 2, :, :]
                                              .rearrange("p h i d -> p (h i d)"), identr[:, :])
                        mm.then_inc(qk_in_psum, 1)


def routing0(nc, io, g):
    with ExitStack() as stack:
        m = Mem(nc, stack, "rt")
        top = m.sb("top", [P, NT, 8])
        row1 = m.sb("row1", [P, NT])
        prob = m.sb("prob", [P, NT, E0])
        rest = m.sb("rest", [P, NT, E0])
        chosen = m.sb("chosen", [P, NT, E0])
        weight = m.sb("weight", [P, NT, E0])
        order = m.sb("order", [P, NT])
        queue = g["queue"]
        zero = m.sb("zero", [P, 17 * XROW])
        scale = m.sb("scale", [P, H1])
        norm = m.sb("norm", [P, H1])
        d_in, scale_ready, wo_ready = (m.sem(n) for n in ("d_in", "scale_ready", "wo_ready"))
        p_s = [m.ps(f"p_s{i}", [E0, 4, P]) for i in range(4)]
        (c_in, prob_ready, chain, sel_ready, sel_in_psum, weight_ready, weight_stored, zeroed, tables_zero, exp_done) = (m.sem(n) for n in (
             "c_in", "prob_ready", "chain", "sel_ready", "sel_in_psum", "weight_ready", "weight_stored",
             "zeroed", "tables_zero", "exp_done"))
        block = stack.enter_context(nc.Block())

        @block.gpsimd
        def _(pool):
            pool.memset(zero[:, :], 0.0).then_inc(zeroed, 1)
            pool.wait_ge(d_in, 32)
            pool.wait_ge(scale_ready, 1)
            pool.tensor_tensor(g["wo1"][:, :, :], g["wo1"][:, :, :], scale[:, :].unsqueeze(2).to_broadcast([P, H1, D]),
                               ALU.mult).then_inc(wo_ready, 1)
            pool.wait_ge(wo_ready, 1)

        @block.sync
        def _(sp):
            sp.dma_start(order[:, :], io["c_order"]).then_inc(c_in, 16)
            sp.dma_start(norm[:, :], io["norm1T"]).then_inc(d_in, 16)
            sp.dma_start(g["wo1"][:, :, :], io["WoT1"].rearrange("(h p) n -> p h n", p=P)).then_inc(d_in, 16)
            sp.wait_ge(zeroed, 1)
            rows = SLOTS0 // P
            for a in g["acc"]:
                sp.dma_start(a.rearrange("(p n) d -> p (n d)", p=P), zero[:, 0:rows * D]).then_inc(tables_zero, 16)
            sp.dma_start(g["xtab"][TOK:SLOTS0, :], zero[:, 0:XROW]).then_inc(tables_zero, 16)
            sp.wait_ge(weight_ready, 1)
            sp.dma_start(g["xtab"][0:TOK, D:XROW].rearrange("(t p) e -> p t e", p=P), weight[:, :, :]).then_inc(weight_stored, 16)
            sp.wait_ge(tables_zero, 16 * (len(g["acc"]) + 1))
            sp.wait_ge(weight_stored, 16)

        @block.vector
        def _(dve):
            n = 0

            def step(ins):
                nonlocal n
                n += 1
                ins.then_inc(chain, 1)
                dve.wait_ge(chain, n)

            logits = g["logits"]
            step(dve.tensor_reduce(row1[:, :], logits[:, :, :], AX_X, ALU.max))
            dve.tensor_tensor(prob[:, :, :], logits[:, :, :], row1[:, :].unsqueeze(2).to_broadcast([P, NT, E0]),
                              ALU.subtract).then_inc(prob_ready, 1)
            dve.wait_ge(exp_done, 1)
            for t in range(NT):
                ins = dve.max(top[:, t, :], prob[:, t, :])
            step(ins)
            for t in range(NT):
                ins = dve.match_replace(rest[:, t, :], top[:, t, :], prob[:, t, :], -1.0)
            step(ins)
            step(dve.tensor_tensor(chosen[:, :, :], prob[:, :, :], rest[:, :, :], ALU.not_equal))
            dve.wait_ge(c_in, 16)
            dve.tensor_tensor(rest[:, :, :], chosen[:, :, :], order[:, :].unsqueeze(2).to_broadcast([P, NT, E0]),
                              ALU.mult).then_inc(sel_ready, 1)
            step(dve.tensor_tensor(weight[:, :, :], prob[:, :, :], chosen[:, :, :], ALU.mult))
            step(dve.tensor_reduce(row1[:, :], weight[:, :, :], AX_X, ALU.add))
            step(dve.reciprocal(row1[:, :], row1[:, :]))
            dve.tensor_tensor(weight[:, :, :], weight[:, :, :], row1[:, :].unsqueeze(2).to_broadcast([P, NT, E0]),
                              ALU.mult).then_inc(weight_ready, 1)
            dve.wait_ge(d_in, 32)
            dve.tensor_scalar(scale[:, :], norm[:, :], 0.5, None, ALU.mult).then_inc(scale_ready, 1)
            for i in range(4):
                dve.wait_ge(sel_in_psum, i + 1)
                ins = dve.tensor_copy(queue[:, i * 4 * P:(i + 1) * 4 * P], p_s[i][:, :, :].rearrange("e a p -> e (a p)"))
            step(ins)

        @block.scalar
        def _(act):
            act.wait_ge(prob_ready, 1)
            act.activation(prob[:, :, :], prob[:, :, :], ACT.Exp).then_inc(exp_done, 1)

        @block.tensor
        def _(pe):
            ident = g["ident"]
            pe.wait_ge(sel_ready, 1)
            for t in range(NT):
                mm = pe.transpose(p_s[t // 4][:, t % 4, :], rest[:, t, :], ident[:, :])
                if t % 4 == 3:
                    mm.then_inc(sel_in_psum, 1)


def attention0(nc, io, g):
    assert CAP // 8 == NT == H1
    KEYS = 2 * P
    STEPS_B = TPB * G0
    HALF = P // 2
    with ExitStack() as stack:
        m = Mem(nc, stack, "at")
        wo = m.sb("wo", [P, KD, D])
        bo = m.sb("bo", [P, D])
        maskf = m.sb("maskf", [P, 2, KEYS])
        mask = m.sb("mask", [P, 2, 2, KEYS], BF16)
        maskTf = m.sb("maskTf", [P, 2 * 2, P])
        maskT = m.sb("maskT", [P, 2 * 2, R0, P], BF16)
        identb = m.sb("identb", [P, P], BF16)
        minus_onesf = m.sb("minus_onesf", [P, P])
        minus_ones = m.sb("minus_ones", [P, P], F32R)
        qs = [m.sb(f"qs{s}", [P, 2, R0 * P], F32R) for s in range(2)]
        kc = [m.sb(f"kc{s}", [P, 2, KEYS], F32R) for s in range(2)]
        vc = [m.sb(f"vc{s}", [P, 2, G0, HD + 1]) for s in range(2)]
        top = [m.sb(f"top{s}", [P, R0]) for s in range(2)]
        diag = [m.sb(f"diag{s}", [P, R0, P], F32R) for s in range(2)]
        pT = [m.sb(f"pT{s}", [P, 2, R0 * P]) for s in range(2)]
        inv = [m.sb(f"inv{s}", [P, H0]) for s in range(2)]
        y = [m.sb(f"y{s}", [P, D]) for s in range(2)]
        yT = [m.sb(f"yT{s}", [P, KD, P]) for s in range(2)]
        lag = g["logits"][:, 0:NT // 2, :].rearrange("p t e -> p (t e)")
        causal = g["logits"][:, NT // 2:NT, :].rearrange("p t e -> p (t e)")
        slope = m.sb("slope", [P, H1])
        rate = m.sb("rate", [P, H1])
        rate_ready, decays_done, causal_done = (m.sem(n) for n in ("rate_ready", "decays_done", "causal_done"))
        row = m.sb("row", [P, 1])
        eight = m.sb("eight", [E0, 8])
        first = m.sb("first", [E0, CAP])
        spare = m.sb("spare", [P, E0])
        lstf = m.sb("lstf", [P, E0])
        picked, listed, removed, list_in_psum, slots_step = (m.sem(n) for n in (
            "picked", "listed", "removed", "list_in_psum", "slots_step"))
        p_s = [m.ps(f"p_s{s}", [P, R0, KEYS]) for s in range(2)]
        p_t = [m.ps(f"p_t{c}", [P, R0 * P]) for c in range(2)]
        p_y = m.ps("p_y", [P, 512])
        p_o = m.ps("p_o", [P, 2, D])
        (w_in, consts_ready, ones_set, base_staged, staged, v_staged, scored, max_done, diag_ready, scoredT, exps_done,
         values_done, inv_ready, y_ready, yT_in_psum, yT_ready, out_in_psum, added) = (m.sem(n) for n in (
             "w_in", "consts_ready", "ones_set", "base_staged", "staged", "v_staged", "scored", "max_done",
             "diag_ready", "scoredT", "exps_done", "values_done", "inv_ready", "y_ready", "yT_in_psum", "yT_ready",
             "out_in_psum", "added"))
        block = stack.enter_context(nc.Block())
        STEPS = STEPS_B + 4
        tile_at = lambda u, after: (u - G0 - after) // G0 if u >= G0 + after and (u - G0 - after) % G0 == 0 else None
        sums = p_y[:, 0:H0 * (HD + 1)].rearrange("p (h d) -> p h d", d=HD + 1)

        @block.sync
        def _(sp):
            sp.dma_start(wo[:, :, :], io["Wo0"].rearrange("(k p) n -> p k n", p=P)).then_inc(w_in, 16)
            sp.dma_start(bo[:, :], io["bo0"].to_broadcast([P, D])).then_inc(w_in, 16)
            sp.dma_start(maskf[:, :, :].rearrange("p a n -> p (a n)"), io["c_mask"]).then_inc(w_in, 16)
            sp.dma_start(maskTf[:, :, :].rearrange("p a n -> p (a n)"), io["c_maskT"]).then_inc(w_in, 16)
            sp.dma_start(row[:, :], io["c_row"]).then_inc(w_in, 16)
            sp.dma_start(lag, io["c_lag"]).then_inc(w_in, 16)
            sp.dma_start(causal, io["c_causal"]).then_inc(w_in, 16)
            sp.dma_start(slope[:, :], io["slope1"].to_broadcast([P, H1])).then_inc(w_in, 16)
            sp.wait_ge(w_in, 128)

        @block.gpsimd
        def _(pool):
            pool.sem_inc(staged, 2)
            pool.memset(minus_onesf[:, :], -1.0).then_inc(ones_set, 1)
            for s in range(2):
                pool.memset(vc[s][:, 0, :, :], 0.0).then_inc(base_staged, 1)
            pool.wait_ge(w_in, 128)
            with pool.Fori(0, BATCH) as b:
                for i in range(TPB):
                    t, s = TPB * b + i, i % 2
                    before = t - 1 if i else t
                    pool.wait_ge(y_ready, freed(t))
                    pool.tensor_tensor(g["x"][:, t, :], g["x"][:, t, :], bo[:, :], ALU.add)
                    pool.tensor_copy(kc[s][:, :, 0:N_META], g["kT"][:, :, bass.ds(TPB * b * P, N_META)])
                    pool.tensor_copy(kc[s][:, :, N_META:P], g["kT"][:, :, bass.ds(before * P + N_META, P - N_META)])
                    pool.tensor_copy(kc[s][:, :, P:KEYS], g["kT"][:, :, bass.ds(t * P, P)])
                    pool.tensor_copy(vc[s][:, 1, :, :], g["V"][:, t, :, :])
                    pool.tensor_copy(qs[s][:, :, :], g["qT"][:, t, :, :]).then_inc(staged, 1)
                    pool.wait_ge(decays_done, t + 1)
                    pool.tensor_tensor(g["decay"][:, t, :], g["decay"][:, t, :], causal, ALU.mult).then_inc(causal_done, 1)
            pool.wait_ge(causal_done, NT)

        @block.tensor
        def _(pe):
            for q in (scored, values_done, yT_in_psum, out_in_psum):
                pe.sem_inc(q, 2)
            pe.sem_inc(scoredT, 4)
            pe.wait_ge(w_in, 128)
            pe.wait_ge(consts_ready, 4)

            def score(b, u):
                i, a, s = u // G0, u % G0 // 2, u % 2
                t, n = TPB * b + i, STEPS_B * b + u
                rows = slice(HALF * s, HALF * (s + 1))
                if u % G0 == 0:
                    pe.wait_ge(staged, ready(t))
                pe.wait_ge(max_done, freed(n))
                flat = p_s[s][:, :, :].rearrange("p g k -> p (g k)")
                for half in range(2):
                    pe.matmul(flat[:, half * 512:(half + 1) * 512], identb[:, :], mask[:, min(i, 1), :, :].rearrange("p a k -> p (a k)"),
                              start=True, stop=False, skip_group_check=True)
                for r in range(R0):
                    mm = pe.matmul(p_s[s][:, r, :], qs[i % 2][rows, a, r * P:(r + 1) * P], kc[i % 2][rows, a, :],
                                   start=False, stop=True, skip_group_check=True)
                mm.then_inc(scored, 1)

            def score_turned(b, u):
                i, a, s = u // G0, u % G0 // 2, u % 2
                n = STEPS_B * b + u
                rows = slice(HALF * s, HALF * (s + 1))
                for c in range(2):
                    pe.wait_ge(exps_done, ready(2 * n + c - 2, 4))
                    pe.matmul(p_t[c][:, :], identb[:, :], maskT[:, 2 * min(i, 1) + c, :, :].rearrange("p r q -> p (r q)"),
                              start=True, stop=False, skip_group_check=True)
                    pe.matmul(p_t[c][:, :], kc[i % 2][rows, a, c * P:(c + 1) * P], qs[i % 2][rows, a, :],
                              start=False, stop=False, skip_group_check=True)
                    if c == 0:
                        pe.wait_ge(diag_ready, ready(n))
                    pe.matmul(p_t[c][:, :], minus_ones[:, :], diag[s][:, :, :].rearrange("p r q -> p (r q)"),
                              start=False, stop=True, skip_group_check=True).then_inc(scoredT, 1)

            def values(b, u):
                i, kv, s = u // G0, u % G0, u % 2
                t, n = TPB * b + i, STEPS_B * b + u
                if kv == 0:
                    pe.wait_ge(v_staged, ready(t))
                    pe.wait_ge(y_ready, ready(t - 1))
                pe.wait_ge(exps_done, ready(2 * n + 1, 4))
                for r in range(R0):
                    for c in range(2):
                        mm = pe.matmul(sums[:, kv * R0 + r, :], pT[s][:, c, r * P:(r + 1) * P], vc[i % 2][:, c, kv, :],
                                       start=c == 0, stop=c == 1)
                mm.then_inc(values_done, 1)

            def turn(b, i):
                t, s = TPB * b + i, i % 2
                pe.wait_ge(y_ready, ready(t))
                pe.wait_ge(added, freed(t + 1))
                for k in range(KD):
                    mm = pe.transpose(p_o[:, 0, k * P:(k + 1) * P], y[s][:, k * P:(k + 1) * P], g["ident"][:, :])
                mm.then_inc(yT_in_psum, 1)

            def project(b, i):
                t, s = TPB * b + i, i % 2
                pe.wait_ge(yT_ready, ready(t))
                for k in range(KD):
                    mm = pe.matmul(p_o[:, 1, :], yT[s][:, k, :], wo[:, k, :], start=k == 0, stop=k == KD - 1)
                mm.then_inc(out_in_psum, 1)

            with pe.Fori(0, BATCH) as b:
                for u in range(STEPS):
                    if u < STEPS_B:
                        score(b, u)
                    if 1 <= u <= STEPS_B:
                        score_turned(b, u - 1)
                    if 2 <= u <= STEPS_B + 1:
                        values(b, u - 2)
                    if tile_at(u, 2) is not None:
                        turn(b, tile_at(u, 2))
                    if tile_at(u, 3) is not None:
                        project(b, tile_at(u, 3))
            pe.wait_ge(listed, NT + 2)
            pe.wait_ge(added, NT + 2)
            pe.transpose(p_o[:, 0, 0:E0], first[:, :], g["ident"][0:E0, 0:E0]).then_inc(list_in_psum, 1)

        @block.scalar
        def _(act):
            act.sem_inc(exps_done, 4)
            act.sem_inc(yT_ready, 2)
            act.wait_ge(rate_ready, 1)
            with act.Fori(0, BATCH) as b:
                for u in range(1, STEPS):
                    if u % G0 == 2 and u < STEPS_B:
                        t = TPB * b + u // G0
                        act.activation(g["decay"][:, t, :], lag, ACT.Exp, scale=rate[:, bass.ds(t, 1)]).then_inc(decays_done, 1)
                    if u <= STEPS_B:
                        s, n = (u - 1) % 2, STEPS_B * b + u - 1
                        act.wait_ge(values_done, freed(n))
                        for c in range(2):
                            act.wait_ge(scoredT, ready(2 * n + c, 4))
                            act.activation(pT[s][:, c, :], p_t[c][:, :], ACT.Exp, scale=HD ** -0.5).then_inc(exps_done, 1)
                    if tile_at(u, 2) is not None:
                        i = tile_at(u, 2)
                        t = TPB * b + i
                        act.wait_ge(yT_in_psum, ready(t))
                        act.wait_ge(out_in_psum, freed(t))
                        act.activation(yT[i % 2][:, :, :].rearrange("p k n -> p (k n)"), p_o[:, 0, :], ACT.Copy)\
                            .then_inc(yT_ready, 1)

        @block.vector
        def _(dve):
            for q in (max_done, diag_ready, inv_ready, y_ready, added, v_staged, picked, listed, removed):
                dve.sem_inc(q, 2)
            dve.wait_ge(w_in, 128)
            dve.wait_ge(ones_set, 1)
            dve.tensor_copy(mask[:, :, :, :], maskf[:, :, :].unsqueeze(2).to_broadcast([P, 2, 2, KEYS])).then_inc(consts_ready, 1)
            dve.tensor_copy(maskT[:, :, :, :], maskTf[:, :, :].unsqueeze(2).to_broadcast([P, 4, R0, P])).then_inc(consts_ready, 1)
            dve.tensor_copy(identb[:, :], g["ident"][:, :]).then_inc(consts_ready, 1)
            dve.tensor_copy(minus_ones[:, :], minus_onesf[:, :]).then_inc(consts_ready, 1)
            dve.tensor_scalar(rate[:, :], slope[:, :], -1.0, None, ALU.mult).then_inc(rate_ready, 1)
            dve.wait_ge(base_staged, 2)
            with dve.Fori(0, BATCH) as b:
                for u in range(STEPS):
                    if u % G0 == 0 and u < STEPS_B:
                        i = u // G0
                        before = TPB * b + max(i - 1, 0)
                        dve.tensor_copy(vc[i % 2][0:N_META, 0, :, :], g["V"][0:N_META, TPB * b, :, :])
                        dve.tensor_copy(vc[i % 2][32:64, 0, :, :], g["V"][32:64, before, :, :])
                        dve.tensor_copy(vc[i % 2][64:P, 0, :, :], g["V"][64:P, before, :, :]).then_inc(v_staged, 1)
                    if u < STEPS_B:
                        s, n = u % 2, STEPS_B * b + u
                        dve.wait_ge(scored, ready(n))
                        dve.tensor_reduce(top[s][:, :], p_s[s][:, :, :], AX_X, ALU.max).then_inc(max_done, 1)
                        dve.wait_ge(max_done, ready(n))
                        dve.wait_ge(scoredT, freed(n, 2))
                        dve.tensor_tensor(diag[s][:, :, :], g["ident"][:, :].unsqueeze(1).to_broadcast([P, R0, P]),
                                          top[s][:, :].unsqueeze(2).to_broadcast([P, R0, P]), ALU.mult).then_inc(diag_ready, 1)
                    if tile_at(u, 1) is not None:
                        i = tile_at(u, 1)
                        t = TPB * b + i
                        dve.wait_ge(removed, ready(t - 1))
                        dve.wait_ge(values_done, ready(STEPS_B * b + G0 * i + G0 - 1))
                        dve.reciprocal(inv[i % 2][:, :], sums[:, :, HD]).then_inc(inv_ready, 1)
                        dve.wait_ge(inv_ready, ready(t))
                        dve.wait_ge(yT_in_psum, freed(t))
                        dve.tensor_tensor(y[i % 2][:, :].rearrange("p (h d) -> p h d", d=HD), sums[:, :, 0:HD],
                                          inv[i % 2][:, :].unsqueeze(2).to_broadcast([P, H0, HD]), ALU.mult).then_inc(y_ready, 1)
                        dve.max(eight[:, :], g["queue"][:, :]).then_inc(picked, 1)
                    if tile_at(u, 2) is not None:
                        t = TPB * b + tile_at(u, 2)
                        dve.wait_ge(picked, ready(t))
                        dve.tensor_copy(first[:, bass.ds(8 * t, 8)], eight[:, :]).then_inc(listed, 1)
                        dve.match_replace(g["queue"][:, :], eight[:, :], g["queue"][:, :], -1.0).then_inc(removed, 1)
                    if tile_at(u, 3) is not None:
                        i = tile_at(u, 3)
                        t = TPB * b + i
                        dve.wait_ge(out_in_psum, ready(t))
                        dve.wait_ge(staged, ready(t))
                        dve.tensor_tensor(g["x"][:, t, :], g["x"][:, t, :], p_o[:, 1, :], ALU.add).then_inc(added, 1)
            dve.wait_ge(added, NT + 2)
            dve.wait_ge(list_in_psum, 1)
            lists = p_o[:, 0, 0:E0]
            dve.tensor_scalar(spare[:, :], lists, 0.0, row[:, 0:1], ALU.is_equal, ALU.mult).then_inc(slots_step, 1)
            dve.wait_ge(slots_step, 1)
            dve.scalar_tensor_tensor(lstf[:, :], lists, -1.0, spare[:, :], ALU.mult, ALU.add).then_inc(slots_step, 1)
            dve.wait_ge(slots_step, 2)
            dve.tensor_scalar(g["slot_token"][:, :], lstf[:, :], float(TOK), None, ALU.add).then_inc(slots_step, 1)
            dve.wait_ge(slots_step, 3)


def experts0(nc, io, g):
    U = 4
    EW = 2 * I0
    assert E0 // U == E1 * KD == E1 * F1 // P // 2
    up1 = g["up1"][:, :, :, :].rearrange("p e k n -> p (e k) n")
    down1 = g["down1"][:, :, :, :].rearrange("p e k n -> p (e k) n")
    with ExitStack() as stack:
        m = Mem(nc, stack, "e0")
        up = [m.sb(f"up{s}", [P, KD, EW]) for s in range(U)]
        down = [m.sb(f"down{s}", [I0, D]) for s in range(U)]
        xe = [m.sb(f"xe{s}", [P, XROW]) for s in range(U)]
        wgt = [m.sb(f"wgt{s}", [P, 1]) for s in range(U)]
        xT = [m.sb(f"xT{s}", [P, KD, P]) for s in range(2)]
        gate = [m.sb(f"gate{s}", [I0, P]) for s in range(2)]
        hT = [m.sb(f"hT{s}", [I0, P]) for s in range(2)]
        ye = [m.sb(f"ye{s}", [P, D]) for s in range(U)]
        p_x = [m.ps(f"p_x{s}", [P, KD, P]) for s in range(2)]
        p_h = [m.ps(f"p_h{s}", [I0, 2, P]) for s in range(2)]
        p_y = [m.ps(f"p_y{s}", [P, D]) for s in range(2)]
        (x_in_psum, xT_ready, h_in_psum, gate_ready, hT_ready, y_in_psum, wgt_ready,
         ye_ready) = (m.sem(n) for n in (
             "x_in_psum", "xT_ready", "h_in_psum", "gate_ready", "hT_ready",
             "y_in_psum", "wgt_ready", "ye_ready"))
        weights_in = [m.sem(f"weights_in{s}") for s in range(U)]
        gathered = [m.sem(f"gathered{s}") for s in range(U)]
        summed = [m.sem(f"summed{s}") for s in range(U)]
        block = stack.enter_context(nc.Block())

        @block.sync
        def _(sp):
            with sp.Fori(0, E0 // U) as j:
                for s in range(U):
                    e = U * j + s
                    sp.wait_ge(y_in_psum, freed(e))
                    sp.dma_start(up[s][:, :, :], io["gate_up0"][bass.ds(e, 1), :, :].rearrange("a (k p) n -> p (a k) n", p=P))\
                        .then_inc(weights_in[s], 16)
                    sp.dma_start(down[s][:, :], io["down0"][bass.ds(e, 1), :, :].rearrange("a i n -> (a i) n"))\
                        .then_inc(weights_in[s], 16)
                sp.dma_start(up1[:, bass.ds(j, 1), :], io["gate_up1"].rearrange("e (k p) n -> (e k) p n", p=P)[bass.ds(j, 1), :, :]
                             .rearrange("a p n -> p a n")).then_inc(g["weights1_in"], 16)
                sp.dma_start(down1[:, bass.ds(2 * j, 2), :], io["down1"].rearrange("e (k p) n -> (e k) p n", p=P)[bass.ds(2 * j, 2), :, :]
                             .rearrange("a p n -> p a n")).then_inc(g["weights1_in"], 16)
            sp.dma_start(up1[:, E1 * KD:, :], io["shared_up1"].rearrange("(k p) n -> p k n", p=P)).then_inc(g["weights1_in"], 16)
            sp.dma_start(down1[:, E1 * F1 // P:, :], io["shared_down1"].rearrange("(k p) n -> p k n", p=P)).then_inc(g["weights1_in"], 16)

        @block.gpsimd
        def _(pool):
            def rows(e):
                return bass.IndirectOffsetOnAxis(g["slot_token"][:, e:e + 1], 0)

            def gather(e):
                s = e % U
                if e >= U:
                    pool.wait_ge(ye_ready, freed(e))
                pool.indirect_dma_start(xe[s][:, :], None, g["xtab"][:, :], rows(e)).then_inc(gathered[s], 16)

            def scatter(e):
                s = e % U
                pool.wait_ge(ye_ready, ready(e, U))
                if e >= 2:
                    pool.wait_ge(summed[(e - 2) % U], 16 * ((e - 2) // U + 1))
                pool.indirect_dma_start(g["acc"][e % 2][:, :], rows(e), ye[s][:, :], None,
                                        compute_op=ALU.add).then_inc(summed[s], 16)

            for e in range(U):
                gather(e)
            for e in range(E0):
                scatter(e)
                if e + U < E0:
                    gather(e + U)
            for s in range(U):
                pool.wait_ge(summed[s], 16 * (E0 // U))

        @block.tensor
        def _(pe):
            for q in (x_in_psum, h_in_psum):
                pe.sem_inc(q, 2)
            pe.sem_inc(y_in_psum, U)
            ident = g["ident"]
            with pe.Fori(0, E0 // U) as j:
                def turn(s):
                    e = U * j + s
                    pe.wait_ge(gathered[s], 16 * (j + 1))
                    pe.wait_ge(xT_ready, freed(e))
                    for k in range(KD):
                        mm = pe.transpose(p_x[s % 2][:, k, :], xe[s][:, k * P:(k + 1) * P], ident[:, :])
                    mm.then_inc(x_in_psum, 1)

                def hidden(s):
                    e = U * j + s
                    pe.wait_ge(weights_in[s], 32 * (j + 1))
                    pe.wait_ge(xT_ready, ready(e))
                    pe.wait_ge(hT_ready, freed(e))
                    for half in range(2):
                        for k in range(KD):
                            mm = pe.matmul(p_h[s % 2][:, half, :], up[s][:, k, half * I0:(half + 1) * I0],
                                           xT[s % 2][:, k, :], start=k == 0, stop=k == KD - 1)
                    mm.then_inc(h_in_psum, 1)

                def output(s):
                    e = U * j + s
                    pe.wait_ge(hT_ready, ready(e))
                    pe.wait_ge(ye_ready, freed(e + 2))
                    pe.matmul(p_y[s % 2][:, :], hT[s % 2][:, :], down[s][:, :], start=True, stop=True).then_inc(y_in_psum, 1)

                for step in range(U + 2):
                    if step < U:
                        turn(step)
                    if 1 <= step <= U:
                        hidden(step - 1)
                    if step >= 2:
                        output(step - 2)

        @block.scalar
        def _(act):
            act.sem_inc(gate_ready, 2)
            act.sem_inc(ye_ready, U)

            def turn(j, first=False):
                for step in range(U + 1):
                    if step < U:
                        s, e = step, U * j + step
                        act.wait_ge(h_in_psum, ready(e))
                        act.wait_ge(hT_ready, freed(e))
                        act.activation(gate[s % 2][:, :], p_h[s % 2][:, 0, :], ACT.Silu).then_inc(gate_ready, 1)
                    if step >= 1:
                        s, e = step - 1, U * j + step - 1
                        act.wait_ge(y_in_psum, ready(e, U))
                        act.wait_ge(wgt_ready, ready(e, U))
                        if not first:
                            act.wait_ge(summed[s], 16 * j)
                        act.activation(ye[s][:, :], p_y[s % 2][:, :], ACT.Copy, scale=wgt[s][:, :]).then_inc(ye_ready, 1)

            turn(0, first=True)
            with act.Fori(1, E0 // U) as j:
                turn(j)

        @block.vector
        def _(dve):
            for q in (xT_ready, hT_ready):
                dve.sem_inc(q, 2)
            dve.sem_inc(wgt_ready, U)
            with dve.Fori(0, E0 // U) as j:
                for step in range(U + 1):
                    if step < U:
                        s, e = step, U * j + step
                        dve.wait_ge(x_in_psum, ready(e))
                        dve.wait_ge(h_in_psum, freed(e))
                        dve.tensor_copy(xT[s % 2][:, :, :], p_x[s % 2][:, :, :]).then_inc(xT_ready, 1)
                        dve.wait_ge(ye_ready, freed(e))
                        dve.tensor_copy(wgt[s][:, :], xe[s][:, bass.ds(D + e, 1)]).then_inc(wgt_ready, 1)
                    if step >= 1:
                        s, e = step - 1, U * j + step - 1
                        dve.wait_ge(gate_ready, ready(e))
                        dve.wait_ge(y_in_psum, freed(e + 2))
                        dve.tensor_tensor(hT[s % 2][:, :], gate[s % 2][:, :], p_h[s % 2][:, 1, :], ALU.mult).then_inc(hT_ready, 1)


def combine0(nc, g):
    with ExitStack() as stack:
        m = Mem(nc, stack, "cb")
        CHUNK = 4
        part = [m.sb(f"part{i}", [P, CHUNK, D]) for i in range(4)]
        loaded = [m.sem(f"loaded{i}") for i in range(4)]
        added = m.sem("added")
        block = stack.enter_context(nc.Block())

        @block.sync
        def _(sp):
            for c in range(NT // CHUNK):
                for i in range(2):
                    if c >= 2:
                        sp.wait_ge(added, 2 * (c - 2) + i + 1)
                    src = g["acc"][i][c * CHUNK * P:(c + 1) * CHUNK * P, :].rearrange("(t p) d -> p t d", p=P)
                    sp.dma_start(part[2 * (c % 2) + i][:, :, :], src).then_inc(loaded[2 * (c % 2) + i], 16)

        @block.vector
        def _(dve):
            for c in range(NT // CHUNK):
                x = g["x"][:, c * CHUNK:(c + 1) * CHUNK, :]
                for i in range(2):
                    dve.wait_ge(loaded[2 * (c % 2) + i], 16 * (c // 2 + 1))
                    if 2 * c + i:
                        dve.wait_ge(added, 2 * c + i)
                    dve.tensor_tensor(x, x, part[2 * (c % 2) + i][:, :, :], ALU.add).then_inc(added, 1)
            dve.wait_ge(added, 2 * NT // CHUNK)


def project1(nc, io, g):
    with ExitStack() as stack:
        m = Mem(nc, stack, "p1")
        w = m.sb("w", [P, KD, E1])
        xn = [m.sb(f"xn{s}", [P, D]) for s in range(2)]
        xT = [m.sb(f"xT{s}", [P, KD, P]) for s in range(2)]
        p_x = [m.ps(f"p_x{s}", [P, KD, P]) for s in range(2)]
        p_r = [m.ps(f"p_r{s}", [P, E1]) for s in range(2)]
        w_in, xn_ready, x_in_psum, xT_ready, routed, logits_kept = (m.sem(n) for n in (
            "w_in", "xn_ready", "x_in_psum", "xT_ready", "routed", "logits_kept"))
        rows_stored = [m.sem(f"rows_stored{s}") for s in range(2)]
        cols_stored = [m.sem(f"cols_stored{s}") for s in range(2)]
        block = stack.enter_context(nc.Block())

        @block.sync
        def _(sp):
            for s in range(2):
                sp.sem_inc(rows_stored[s], 16)
                sp.sem_inc(cols_stored[s], 16)
            sp.dma_start(w[:, :, :], io["routerT1"].rearrange("(k p) n -> p k n", p=P)).then_inc(w_in, 16)
            with sp.Fori(0, NT // 2) as j:
                for s in range(2):
                    t = 2 * j + s
                    sp.wait_ge(xT_ready, ready(t))
                    sp.wait_ge(xn_ready, ready(t))
                    sp.dma_start(g["rows1"][bass.ds(RT1 * P + t * P, P), :], xn[s][:, :]).then_inc(rows_stored[s], 16)
                    sp.dma_start(g["cols1"][:, :, bass.ds(t * P, P)], xT[s][:, :, :]).then_inc(cols_stored[s], 16)
            for s in range(2):
                sp.wait_ge(rows_stored[s], 16 * (NT // 2 + 1))
                sp.wait_ge(cols_stored[s], 16 * (NT // 2 + 1))

        @block.vector
        def _(dve):
            dve.sem_inc(xn_ready, 2)
            with dve.Fori(0, NT // 2) as j:
                for s in range(2):
                    t = 2 * j + s
                    dve.wait_ge(x_in_psum, freed(t))
                    dve.wait_ge(rows_stored[s], freed(j, 16))
                    dve.tensor_scalar(xn[s][:, :], g["x"][:, t, :], g["norm"][:, t, 0:1], g["norm"][:, t, 1:2],
                                      ALU.subtract, ALU.mult).then_inc(xn_ready, 1)

        @block.scalar
        def _(act):
            act.sem_inc(xT_ready, 2)
            act.sem_inc(logits_kept, 2)
            with act.Fori(0, NT // 2) as j:
                for s in range(2):
                    t = 2 * j + s
                    act.wait_ge(x_in_psum, ready(t))
                    act.wait_ge(routed, freed(t))
                    act.wait_ge(cols_stored[s], freed(j, 16))
                    act.activation(xT[s][:, :, :], p_x[s][:, :, :], ACT.Copy).then_inc(xT_ready, 1)
                for s in range(2):
                    t = 2 * j + s
                    act.wait_ge(routed, ready(t))
                    act.activation(g["logits1"][:, t, :], p_r[s][:, :], ACT.Copy).then_inc(logits_kept, 1)
            act.wait_ge(logits_kept, NT + 2)

        @block.tensor
        def _(pe):
            pe.sem_inc(x_in_psum, 2)
            pe.sem_inc(routed, 2)
            pe.wait_ge(w_in, 16)
            with pe.Fori(0, NT // 2) as j:
                for s in range(2):
                    t = 2 * j + s
                    pe.wait_ge(xn_ready, ready(t))
                    pe.wait_ge(xT_ready, freed(t))
                    for k in range(KD):
                        mm = pe.transpose(p_x[s][:, k, :], xn[s][:, k * P:(k + 1) * P], g["ident"][:, :])
                    mm.then_inc(x_in_psum, 1)
                for s in range(2):
                    t = 2 * j + s
                    pe.wait_ge(xT_ready, ready(t))
                    pe.wait_ge(logits_kept, freed(t))
                    for k in range(KD):
                        mm = pe.matmul(p_r[s][:, :], xT[s][:, k, :], w[:, k, :], start=k == 0, stop=k == KD - 1)
                    mm.then_inc(routed, 1)


def routing1(nc, io, g):
    with ExitStack() as stack:
        m = Mem(nc, stack, "r1")
        tri = m.sb("tri", [P, P])
        ones = m.sb("ones", [P, P])
        prefer = m.sb("prefer", [P, E1])
        starts = m.sb("starts", [P, RT1, E1])
        best = m.sb("best", [P, NT])
        gate = m.sb("gate", [P, NT])
        rgate = m.sb("rgate", [P, NT])
        cand = m.sb("cand", [P, NT, E1])
        chosen = m.sb("chosen", [P, NT, E1])
        counts = m.sb("counts", [P, E1, NT])
        until = m.sb("until", [P, E1, NT])
        n_e = m.sb("n_e", [P, E1])
        n_i = m.sb("n_i", [P, E1], I32)
        room = m.sb("room", [P, E1])
        end = m.sb("end", [P, E1])
        shift = m.sb("shift", [P, E1])
        full = m.sb("full", [P, RT1, E1])
        passed = m.sb("passed", [P, RT1])
        slotf = m.sb("slotf", [P, NT])
        xs = [m.sb(f"xs{s}", [P, D]) for s in range(2)]
        row_out = [m.sb(f"row_out{s}", [P, 1], U32) for s in range(2)]
        zero = m.sb("zero", [P, RT1 * D // 2])
        p_r = m.ps("p_r", [P, NT, E1])
        p_n = m.ps("p_n", [P, NT, E1])
        c_in, chain, chosen_ready, ranked, best_ready, gate_ready, zeroed, cleared, slots_ready, xs_ready, row_ready = (
            m.sem(n) for n in ("c_in", "chain", "chosen_ready", "ranked", "best_ready", "gate_ready", "zeroed",
                               "cleared", "slots_ready", "xs_ready", "row_ready"))
        scattered = [m.sem(f"scattered{s}") for s in range(2)]
        block = stack.enter_context(nc.Block())

        @block.sync
        def _(sp):
            sp.dma_start(tri[:, :], io["c_tri"]).then_inc(c_in, 16)
            sp.dma_start(prefer[:, :], io["c_prefer"]).then_inc(c_in, 16)
            sp.dma_start(starts[:, :, :].rearrange("p t e -> p (t e)"), io["c_starts"]).then_inc(c_in, 16)
            sp.wait_ge(zeroed, 2)
            v = g["rows1"][0:RT1 * P, :].rearrange("(p n) d -> p (n d)", p=P)
            for half in range(2):
                w = RT1 * D // 2
                sp.dma_start(v[:, half * w:(half + 1) * w], zero[:, :]).then_inc(cleared, 16)
            sp.wait_ge(cleared, 32)

        @block.scalar
        def _(act):
            act.wait_ge(best_ready, 1)
            act.activation(gate[:, :], best[:, :], ACT.Sigmoid).then_inc(gate_ready, 1)

        @block.tensor
        def _(pe):
            pe.wait_ge(c_in, 48)
            pe.wait_ge(zeroed, 2)
            pe.wait_ge(chosen_ready, 1)
            flat = lambda a: a[:, :, :].rearrange("p t e -> p (t e)")
            pe.matmul(flat(p_r), tri[:, :], flat(chosen), start=True, stop=True)
            pe.matmul(flat(p_n), ones[:, :], flat(chosen), start=True, stop=True).then_inc(ranked, 1)

        @block.vector
        def _(dve):
            n = 0

            def step(ins):
                nonlocal n
                n += 1
                ins.then_inc(chain, 1)
                dve.wait_ge(chain, n)

            logits = g["logits1"]
            wide = lambda a: a[:, :].unsqueeze(2).to_broadcast([P, NT, E1])
            dve.tensor_reduce(best[:, :], logits[:, :, :], AX_X, ALU.max).then_inc(best_ready, 1)
            dve.wait_ge(best_ready, 1)
            dve.wait_ge(c_in, 48)
            step(dve.tensor_tensor(cand[:, :, :], logits[:, :, :], wide(best), ALU.is_equal))
            step(dve.tensor_tensor(cand[:, :, :], cand[:, :, :], prefer[:, :].unsqueeze(1).to_broadcast([P, NT, E1]), ALU.mult))
            step(dve.tensor_reduce(slotf[:, :], cand[:, :, :], AX_X, ALU.max))
            dve.tensor_tensor(chosen[:, :, :], cand[:, :, :], wide(slotf), ALU.is_equal).then_inc(chosen_ready, 1)
            dve.wait_ge(ranked, 1)
            step(dve.tensor_copy(counts[:, :, :], p_n[:, :, :].rearrange("p t e -> p e t")))
            flat = lambda a: a[:, :, :].rearrange("p e t -> p (e t)")
            step(dve.tensor_tensor_scan(flat(until), ones[:, :], flat(counts), 0.0, ALU.mult, ALU.add))
            step(dve.tensor_tensor(until[:, :, :], until[:, :, :], counts[:, :, :], ALU.subtract))
            step(dve.tensor_reduce(n_e[:, :], counts[:, :, :], AX_X, ALU.add))
            step(dve.tensor_scalar(n_i[:, :], n_e[:, :], float(P - 1), None, ALU.add))
            step(dve.tensor_scalar(n_i[:, :], n_i[:, :], 7, 7, ALU.arith_shift_right, ALU.arith_shift_left))
            step(dve.tensor_copy(room[:, :], n_i[:, :]))
            step(dve.tensor_tensor_scan(end[:, :], ones[:, 0:E1], room[:, :], 0.0, ALU.mult, ALU.add))
            step(dve.tensor_tensor(shift[:, :], end[:, :], room[:, :], ALU.subtract))
            step(dve.tensor_tensor(shift[:, :], shift[:, :], until[:, :, 0], ALU.subtract))
            step(dve.tensor_tensor(until[:, :, :], until[:, :, :], shift[:, :].unsqueeze(2).to_broadcast([P, E1, NT]), ALU.add))
            step(dve.tensor_tensor(cand[:, :, :], p_r[:, :, :], until[:, :, :].rearrange("p e t -> p t e"), ALU.add))
            step(dve.tensor_tensor(cand[:, :, :], cand[:, :, :], chosen[:, :, :], ALU.mult))
            step(dve.tensor_reduce(slotf[:, :], cand[:, :, :], AX_X, ALU.add))
            dve.tensor_scalar(g["slot1"][:, :], slotf[:, :], -1.0, None, ALU.add).then_inc(slots_ready, 1)
            step(dve.tensor_tensor(full[:, :, :], starts[:, :, :], end[:, :].unsqueeze(1).to_broadcast([P, RT1, E1]), ALU.is_ge))
            step(dve.tensor_reduce(passed[:, :], full[:, :, :], AX_X, ALU.add))
            step(dve.tensor_scalar(g["tile_expert"][0:1, 0:RT1], passed[0:1, :], float(E1 - 1), None, ALU.min))
            step(dve.memset(g["tile_expert"][0:1, RT1:RT1 + NT], E1))
            dve.wait_ge(gate_ready, 1)
            dve.sem_inc(xs_ready, 2)
            step(dve.tensor_tensor(rgate[:, :], gate[:, :], g["norm"][:, :, 1], ALU.mult))
            for t in range(NT):
                s = t % 2
                if t >= 2:
                    dve.wait_ge(scattered[s], 16 * (t // 2))
                dve.tensor_scalar(xs[s][:, :], g["x"][:, t, :], g["norm"][:, t, 0:1], rgate[:, t:t + 1],
                                  ALU.subtract, ALU.mult).then_inc(xs_ready, 1)

        @block.gpsimd
        def _(pool):
            pool.memset(zero[:, :], 0.0).then_inc(zeroed, 1)
            pool.memset(ones[:, :], 1.0).then_inc(zeroed, 1)
            pool.wait_ge(slots_ready, 1)
            pool.wait_ge(cleared, 32)
            for t in range(NT):
                s = t % 2
                pool.wait_ge(xs_ready, ready(t))
                pool.indirect_dma_start(g["rows1"][:, :], bass.IndirectOffsetOnAxis(g["slot1"][:, t:t + 1], 0),
                                        xs[s][:, :], None).then_inc(scattered[s], 16)
            for s in range(2):
                pool.wait_ge(scattered[s], 16 * (NT // 2))


def experts1(nc, io, g):
    HC = F1 // P
    with ExitStack() as stack:
        m = Mem(nc, stack, "e1")
        up, down = g["up1"], g["down1"]
        xe = [m.sb(f"xe{s}", [P, D]) for s in range(2)]
        xT = [m.sb(f"xT{s}", [P, KD, P]) for s in range(2)]
        gate = [m.sb(f"gate{s}", [P, F1]) for s in range(2)]
        h = [m.sb(f"h{s}", [P, F1]) for s in range(2)]
        hT = [m.sb(f"hT{s}", [P, HC, P]) for s in range(2)]
        ye = [m.sb(f"ye{s}", [P, D]) for s in range(2)]
        p_x = m.ps("p_x", [P, KD, P])
        p_g = [m.ps(f"p_g{s}", [P, F1]) for s in range(2)]
        p_u = [m.ps(f"p_u{s}", [P, F1]) for s in range(2)]
        p_h = m.ps("p_h", [P, HC, P])
        p_y = [m.ps(f"p_y{s}", [P, D]) for s in range(2)]
        x_in_psum, xT_ready, up_done, gate_ready, h_ready, h_in_psum, hT_ready, y_in_psum, ye_ready = (
            m.sem(n) for n in ("x_in_psum", "xT_ready", "up_done", "gate_ready", "h_ready", "h_in_psum", "hT_ready",
                               "y_in_psum", "ye_ready"))
        xe_in = [m.sem(f"xe_in{s}") for s in range(2)]
        ye_stored = [m.sem(f"ye_stored{s}") for s in range(2)]
        weights_in = g["weights1_in"]
        block = stack.enter_context(nc.Block())

        @block.sync
        def _(sp):
            with sp.Fori(0, (RT1 + NT) // 2) as j:
                for s in range(2):
                    t = 2 * j + s
                    sp.wait_ge(x_in_psum, freed(t))
                    sp.dma_start(xe[s][:, :], g["rows1"][bass.ds(t * P, P), :]).then_inc(xe_in[s], 16)

        @block.gpsimd
        def _(pool):
            with pool.Fori(0, (RT1 + NT) // 2) as j:
                for s in range(2):
                    t = 2 * j + s
                    pool.wait_ge(ye_ready, ready(t))
                    pool.dma_start(g["out1"][bass.ds(t * P, P), :], ye[s][:, :]).then_inc(ye_stored[s], 16)
            for s in range(2):
                pool.wait_ge(ye_stored[s], 16 * ((RT1 + NT) // 2))

        @block.tensor
        def _(pe):
            for q in (x_in_psum, up_done, h_in_psum, y_in_psum):
                pe.sem_inc(q, 2)

            def turn(t, s, j):
                pe.wait_ge(xe_in[s], 16 * (j + 1))
                pe.wait_ge(xT_ready, freed(t + 1))
                for k in range(KD):
                    mm = pe.transpose(p_x[:, k, :], xe[s][:, k * P:(k + 1) * P], g["ident"][:, :])
                mm.then_inc(x_in_psum, 1)

            def hidden(t, s):
                e = pe.value_load(g["tile_expert"][0:1, bass.ds(t, 1)], min_val=0, max_val=E1)
                pe.wait_ge(xT_ready, ready(t))
                pe.wait_ge(h_ready, freed(t))
                for half, p in enumerate((p_g, p_u)):
                    for k in range(KD):
                        mm = pe.matmul(p[s][:, :], xT[s][:, k, :], up[:, bass.ds(e, 1), k, half * F1:(half + 1) * F1]
                                       .rearrange("p a n -> p (a n)"), start=k == 0, stop=k == KD - 1)
                mm.then_inc(up_done, 1)
                return e

            def turn_hidden(t, s):
                pe.wait_ge(h_ready, ready(t))
                pe.wait_ge(hT_ready, freed(t + 1))
                for c in range(HC):
                    mm = pe.transpose(p_h[:, c, :], h[s][:, c * P:(c + 1) * P], g["ident"][:, :])
                mm.then_inc(h_in_psum, 1)

            def output(t, s, e):
                pe.wait_ge(hT_ready, ready(t))
                pe.wait_ge(ye_ready, freed(t))
                for c in range(HC):
                    mm = pe.matmul(p_y[s][:, :], hT[s][:, c, :], down[:, bass.ds(e, 1), c, :].rearrange("p a n -> p (a n)"),
                                   start=c == 0, stop=c == HC - 1)
                mm.then_inc(y_in_psum, 1)

            pe.wait_ge(weights_in, g["weights1_n"])
            with pe.Fori(0, (RT1 + NT) // 2) as j:
                a, b = 2 * j, 2 * j + 1
                turn(a, 0, j)
                turn(b, 1, j)
                ea = hidden(a, 0)
                eb = hidden(b, 1)
                turn_hidden(a, 0)
                output(a, 0, ea)
                turn_hidden(b, 1)
                output(b, 1, eb)

        @block.scalar
        def _(act):
            for q in (gate_ready, hT_ready):
                act.sem_inc(q, 2)
            with act.Fori(0, (RT1 + NT) // 2) as j:
                for s in range(2):
                    t = 2 * j + s
                    act.wait_ge(up_done, ready(t))
                    act.wait_ge(h_ready, freed(t))
                    act.activation(gate[s][:, :], p_g[s][:, :], ACT.Silu).then_inc(gate_ready, 1)
                for s in range(2):
                    t = 2 * j + s
                    act.wait_ge(h_in_psum, ready(t))
                    act.wait_ge(y_in_psum, freed(t))
                    act.activation(hT[s][:, :, :], p_h[:, :, :], ACT.Copy).then_inc(hT_ready, 1)

        @block.vector
        def _(dve):
            for q in (xT_ready, h_ready, ye_ready):
                dve.sem_inc(q, 2)

            def body(j, first=False):
                for s in range(2):
                    t = 2 * j + s
                    dve.wait_ge(x_in_psum, ready(t))
                    dve.wait_ge(up_done, freed(t))
                    dve.tensor_copy(xT[s][:, :, :], p_x[:, :, :]).then_inc(xT_ready, 1)
                for s in range(2):
                    t = 2 * j + s
                    dve.wait_ge(gate_ready, ready(t))
                    dve.wait_ge(h_in_psum, freed(t))
                    dve.tensor_tensor(h[s][:, :], gate[s][:, :], p_u[s][:, :], ALU.mult).then_inc(h_ready, 1)
                for s in range(2):
                    t = 2 * j + s
                    dve.wait_ge(y_in_psum, ready(t))
                    if not first:
                        dve.wait_ge(ye_stored[s], 16 * j)
                    dve.tensor_copy(ye[s][:, :], p_y[s][:, :]).then_inc(ye_ready, 1)

            body(0, first=True)
            with dve.Fori(1, (RT1 + NT) // 2) as j:
                body(j)


def gather1(nc, g):
    with ExitStack() as stack:
        m = Mem(nc, stack, "g1")
        routed = m.sb("routed", [P, NT, D])
        shared = m.sb("shared", [P, NT, D])
        routed_in, shared_in, added = (m.sem(n) for n in ("routed_in", "shared_in", "added"))
        block = stack.enter_context(nc.Block())

        @block.sync
        def _(sp):
            sp.dma_start(shared[:, :, :], g["out1"][RT1 * P:(RT1 + NT) * P, :].rearrange("(t p) d -> p t d", p=P)).then_inc(shared_in, 16)

        @block.gpsimd
        def _(pool):
            for t in range(NT):
                pool.indirect_dma_start(routed[:, t, :], None, g["out1"][:, :],
                                        bass.IndirectOffsetOnAxis(g["slot1"][:, t:t + 1], 0)).then_inc(routed_in, 16)

        @block.vector
        def _(dve):
            dve.wait_ge(shared_in, 16)
            dve.tensor_tensor(g["x"][:, :, :], g["x"][:, :, :], shared[:, :, :], ALU.add).then_inc(added, 1)
            dve.wait_ge(added, 1)
            dve.wait_ge(routed_in, 16 * NT)
            dve.tensor_tensor(g["x"][:, :, :], g["x"][:, :, :], routed[:, :, :], ALU.add).then_inc(added, 1)
            dve.wait_ge(added, 2)


def attention1(nc, io, g, out):
    DB = SEQ // P
    with ExitStack() as stack:
        m = Mem(nc, stack, "a1")
        xT = m.sb("xT", [P, KD, SEQ])
        w = [m.sb(f"w{s}", [P, KD, 4 * DH1]) for s in range(2)]
        xr = m.sb("xr", [P, 2, KD, SEQ], F32R)
        wr = [m.sb(f"wr{s}", [P, 2, KD, 4 * DH1], F32R) for s in range(2)]
        w_high, w_parts, x_high, x_parts = (m.sem(n) for n in ("w_high", "w_parts", "x_high", "x_parts"))
        q = [m.sb(f"q{s}", [P, SEQ]) for s in range(2)]
        k = [m.sb(f"k{s}", [P, SEQ]) for s in range(2)]
        v = [m.sb(f"v{s}", [P, DB, DH1]) for s in range(2)]
        th = [m.sb(f"th{s}", [P, SEQ]) for s in range(2)]
        sc = [m.sb(f"sc{s}", [P, DB, SEQ]) for s in range(2)]
        sq = [m.sb(f"sq{s}", [P, SEQ]) for s in range(2)]
        sqsum = m.sb("sqsum", [P, SEQ])
        ones = m.sb("ones", [P, 1])
        gated = m.sb("gated", [P, H1, SEQ])
        ms = m.sb("ms", [P, DB])
        rms = m.sb("rms", [P, DB])
        y = m.sb("y", [P, DB, D])
        p_p = [m.ps(f"p_p{s}", [P, SEQ]) for s in range(2)]
        p_s = [m.ps(f"p_s{s}", [P, SEQ]) for s in range(2)]
        p_o = [m.ps(f"p_o{s}", [P, SEQ]) for s in range(2)]
        p_w = [m.ps(f"p_w{s}", [P, 2, D]) for s in range(2)]
        names = ("x_in", "projected", "activated", "scored", "decayed", "out_in_psum", "squared", "summed", "gated_ready",
                 "sum_in_psum", "mean_ready", "root_ready", "rms_ready", "rows_in_psum", "y_ready", "y_stored", "ones_ready")
        (x_in, projected, activated, scored, decayed, out_in_psum, squared, summed, gated_ready, sum_in_psum,
         mean_ready, root_ready, rms_ready, rows_in_psum, y_ready, y_stored, ones_ready) = (m.sem(n) for n in names)
        w_in = [m.sem(f"w_in{s}") for s in range(2)]
        block = stack.enter_context(nc.Block())
        HP = H1 // 2
        TERMS = [(kk, xp, wp) for kk in range(KD) for xp, wp in ((0, 0), (0, 1), (1, 0))]

        @block.sync
        def _(sp):
            sp.sem_inc(y_stored, 16)

            def load(row, s):
                sp.dma_start(w[s][:, :, :], io["Wh1"][bass.ds(row, D), :].rearrange("(k p) n -> p k n", p=P)).then_inc(w_in[s], 16)

            for s in range(2):
                load(s * D, s)
            with sp.Fori(0, BATCH) as b:
                first = sp.snap(b * SEQ)
                sp.wait_ge(projected, 4 * H1 * b + 8)
                sp.dma_start(xT[:, :, :], g["cols1"][:, :, bass.ds(first, SEQ)]).then_inc(x_in, 16)
                with sp.Fori(1, HP) as j:
                    for s in range(2):
                        h = 2 * j + s
                        row = sp.snap(h * D)
                        sp.wait_ge(projected, freed(H1 * b + h, 4))
                        load(row, s)
                for s in range(2):
                    sp.wait_ge(projected, freed(H1 * (b + 1) + s, 4))
                    load(s * D, s)
                sp.wait_ge(y_ready, b + 1)
                sp.dma_start(out[bass.ds(b * SEQ, SEQ), :].rearrange("(t p) d -> p t d", p=P), y[:, :, :]).then_inc(y_stored, 16)
            sp.wait_ge(y_stored, 16 * (BATCH + 1))

        @block.tensor
        def _(pe):
            for sem in (scored, out_in_psum):
                pe.sem_inc(sem, 2)
            pe.sem_inc(projected, 8)
            pe.wait_ge(ones_ready, 1)

            def project(b, pair, s, scores=None):
                n = H1 * b + 2 * pair + s
                pe.wait_ge(w_parts, ready(n))
                for c in range(4):
                    if c == 3 and scores is not None:
                        for i in range(2):
                            score(b, scores, 1 - s, i)
                    pe.wait_ge(activated, freed(4 * n + c))
                    bank = p_p[c % 2]
                    if c == 2:
                        for t in range(DB):
                            for kk in range(KD):
                                mm = pe.matmul(bank[:, t * P:(t + 1) * P], xT[:, kk, t * P:(t + 1) * P],
                                               w[s][:, kk, c * P:(c + 1) * P], start=kk == 0, stop=kk == KD - 1)
                    else:
                        for kk, xp, wp in TERMS:
                            mm = pe.matmul(bank[:, :], wr[s][:, wp, kk, c * P:(c + 1) * P], xr[:, xp, kk, :],
                                           start=(kk, xp, wp) == TERMS[0], stop=(kk, xp, wp) == TERMS[-1])
                    mm.then_inc(projected, 1)

            def score(b, h, s, c):
                n = H1 * b + h
                if c == 0:
                    pe.wait_ge(activated, ready(4 * n + 1))
                pe.wait_ge(decayed, freed(4 * n + c))
                pe.matmul(p_s[c % 2][:, 0:SEQ - c * P], k[s][:, c * P:(c + 1) * P], q[s][:, c * P:SEQ],
                          start=True, stop=True).then_inc(scored, 1)

            def attend(b, h, s):
                n = H1 * b + h
                for c in range(DB):
                    if c == 0:
                        pe.wait_ge(activated, ready(4 * n + 2))
                        pe.wait_ge(gated_ready, freed(n))
                        pe.wait_ge(squared, freed(n))
                    pe.wait_ge(decayed, ready(4 * n + c))
                    mm = pe.matmul(p_o[s][:, c * P:SEQ], v[s][:, c, :], sc[s][:, c, 0:SEQ - c * P],
                                   start=c == 0, stop=c == DB - 1)
                    if c + 2 < DB:
                        score(b, h, s, c + 2)
                mm.then_inc(out_in_psum, 1)

            with pe.Fori(0, BATCH) as b:
                pe.wait_ge(x_parts, b + 2)
                project(b, 0, 0)
                with pe.Fori(0, HP - 1) as j:
                    project(b, j, 1, scores=2 * j)
                    attend(b, 2 * j, 0)
                    project(b, j + 1, 0, scores=2 * j + 1)
                    attend(b, 2 * j + 1, 1)
                project(b, HP - 1, 1, scores=H1 - 2)
                attend(b, H1 - 2, 0)
                for c in range(2):
                    score(b, H1 - 1, 1, c)
                attend(b, H1 - 1, 1)
                pe.wait_ge(gated_ready, ready(H1 * b + H1 - 1))
                for t in range(DB):
                    for h in range(H1):
                        mm = pe.matmul(p_w[t // 2][:, t % 2, :], gated[:, h, t * P:(t + 1) * P], g["wo1"][:, h, :],
                                       start=h == 0, stop=h == H1 - 1)
                mm.then_inc(rows_in_psum, 1)
                pe.wait_ge(summed, H1 * (b + 1) + 2)
                pe.wait_ge(squared, ready(H1 * b + H1 - 1))
                for t in range(DB):
                    mm = pe.matmul(p_o[0][:, t:t + 1], sqsum[:, t * P:(t + 1) * P], ones[:, :], start=True, stop=True)
                mm.then_inc(sum_in_psum, 1)
                pe.wait_ge(rms_ready, b + 1)
                pe.wait_ge(y_ready, b + 1)

        @block.scalar
        def _(act):
            act.sem_inc(activated, 2)
            act.sem_inc(squared, 2)

            def activate(b, h, s):
                n = H1 * b + h
                for c in range(4):
                    act.wait_ge(projected, 4 * n + c + 9)
                    bank = p_p[c % 2]
                    if c == 0:
                        act.wait_ge(out_in_psum, freed(n))
                        act.wait_ge(gated_ready, freed(n))
                    dst = (q[s][:, :], k[s][:, :], v[s][:, :, :].rearrange("p t e -> p (t e)"), th[s][:, :])[c]
                    if c < 3:
                        act.activation(dst, bank[:, :], ACT.Silu).then_inc(activated, 1)
                    else:
                        act.activation(dst, bank[:, :], ACT.Tanh, scale=0.5).then_inc(activated, 1)

            def square(b, h, s):
                n = H1 * b + h
                act.wait_ge(out_in_psum, ready(n))
                act.wait_ge(summed, freed(n))
                act.activation(sq[s][:, :], p_o[s][:, :], ACT.Square).then_inc(squared, 1)

            with act.Fori(0, BATCH) as b:
                activate(b, 0, 0)
                with act.Fori(0, HP - 1) as j:
                    activate(b, 2 * j + 1, 1)
                    square(b, 2 * j, 0)
                    activate(b, 2 * j + 2, 0)
                    square(b, 2 * j + 1, 1)
                activate(b, H1 - 1, 1)
                square(b, H1 - 2, 0)
                square(b, H1 - 1, 1)
                act.wait_ge(mean_ready, b + 1)
                act.activation(rms[:, :], ms[:, :], ACT.Sqrt).then_inc(root_ready, 1)

        @block.gpsimd
        def _(pool):
            pool.memset(ones[:, :], 1.0).then_inc(ones_ready, 1)
            pool.sem_inc(summed, 2)
            pool.sem_inc(w_parts, 2)

            def low(n, s):
                pool.wait_ge(w_high, n + 1)
                pool.tensor_tensor(wr[s][:, 1, :, :], w[s][:, :, :], wr[s][:, 0, :, :], ALU.subtract).then_inc(w_parts, 1)

            low(0, 0)
            low(1, 1)
            with pool.Fori(0, BATCH) as b:
                low(H1 * b + 2, 0)
                low(H1 * b + 3, 1)
                pool.wait_ge(sum_in_psum, b + 1)
                pool.wait_ge(squared, ready(H1 * b + 1))
                pool.tensor_tensor(sqsum[:, :], sq[0][:, :], sq[1][:, :], ALU.add).then_inc(summed, 2)
                with pool.Fori(1, HP) as j:
                    for s in range(2):
                        n = H1 * b + 2 * j + s
                        low(n + 2, s)
                        pool.wait_ge(squared, ready(n))
                        pool.wait_ge(summed, freed(n + 1))
                        pool.tensor_tensor(sqsum[:, :], sqsum[:, :], sq[s][:, :], ALU.add).then_inc(summed, 1)

        @block.vector
        def _(dve):
            dve.sem_inc(decayed, 2)
            dve.sem_inc(gated_ready, 2)
            dve.sem_inc(sum_in_psum, 1)
            dve.sem_inc(x_parts, 1)

            def high(n, m, s):
                dve.wait_ge(w_in[s], 16 * (m + 1))
                dve.wait_ge(projected, freed(n, 4))
                dve.tensor_copy(wr[s][:, 0, :, :], w[s][:, :, :]).then_inc(w_high, 1)

            for s in range(2):
                high(s, 0, s)

            def attend(b, h, s):
                n = H1 * b + h
                for c in range(DB):
                    dve.wait_ge(scored, ready(4 * n + c))
                    if c == 0:
                        dve.wait_ge(out_in_psum, freed(n))
                    width = SEQ - c * P
                    dve.tensor_tensor(sc[s][:, c, 0:width], p_s[c % 2][:, 0:width], g["decay"][:, h, 0:width],
                                      ALU.mult).then_inc(decayed, 1)
                dve.wait_ge(out_in_psum, ready(n))
                dve.wait_ge(activated, ready(4 * n + 3))
                dve.wait_ge(squared, ready(n))
                dve.scalar_tensor_tensor(gated[:, h, :], th[s][:, :], 1.0, p_o[s][:, :], ALU.add, ALU.mult).then_inc(gated_ready, 1)

            with dve.Fori(0, BATCH) as b:
                dve.wait_ge(x_in, 16 * (b + 1))
                dve.wait_ge(projected, 4 * H1 * b + 8)
                dve.tensor_copy(xr[:, 0, :, :], xT[:, :, :]).then_inc(x_high, 1)
                dve.wait_ge(x_high, b + 1)
                dve.tensor_tensor(xr[:, 1, :, :], xT[:, :, :], xr[:, 0, :, :], ALU.subtract).then_inc(x_parts, 1)
                with dve.Fori(0, HP) as j:
                    for s in range(2):
                        high(H1 * b + 2 * j + s + 2, HP * b + j + 1, s)
                        attend(b, 2 * j + s, s)
                dve.wait_ge(sum_in_psum, b + 2)
                dve.tensor_scalar(ms[:, :], p_o[0][:, 0:DB], 1.0 / (H1 * DH1), RMS_EPS, ALU.mult, ALU.add).then_inc(mean_ready, 1)
                dve.wait_ge(root_ready, b + 1)
                dve.reciprocal(rms[:, :], rms[:, :]).then_inc(rms_ready, 1)
                dve.wait_ge(rms_ready, b + 1)
                dve.wait_ge(rows_in_psum, b + 1)
                dve.wait_ge(y_stored, freed(b, 16))
                for t in range(DB):
                    ins = dve.scalar_tensor_tensor(y[:, t, :], p_w[t // 2][:, t % 2, :], rms[:, t:t + 1],
                                                   g["x"][:, DB * b + t, :], ALU.mult, ALU.add)
                ins.then_inc(y_ready, 1)


def program(nc, io, out, upto=99):
    dr = lambda name, shape, dt=F32: nc.dram_tensor(name, shape, dt, kind="Internal").ap()
    with ExitStack() as stack:
        m = Mem(nc, stack, "g")
        g = {
            "ident": m.sb("ident", [P, P]),
            "x": m.sb("x", [P, NT, D]),
            "norm": m.sb("norm", [P, NT, 2]),
            "xtab": dr("xtab", [SLOTS0, XROW]),
            "acc": [dr(f"acc{i}", [SLOTS0, D]) for i in range(2)],
            "rows1": dr("rows1", [(RT1 + NT) * P, D]),
            "out1": dr("out1", [(RT1 + NT) * P, D]),
            "cols1": dr("cols1", [P, KD, TOK]),
            "slot1": m.sb("slot1", [P, NT], U32),
            "tile_expert": m.sb("tile_expert", [1, RT1 + NT], I32),
            "logits1": m.sb("logits1", [P, NT, E1]),
            "slot_token": m.sb("slot_token", [P, E0], U32),
            "decay": m.sb("decay", [P, H1, SEQ]),
            "wo1": m.sb("wo1", [P, H1, D]),
        }
        x_loaded = m.sem("x_loaded")
        with nc.Block() as block:
            @block.sync
            def _(sp):
                x_v = io["x"].rearrange("(t p) d -> p t d", p=P)
                for i in range(4):
                    sp.dma_start(g["x"][:, 4 * i:4 * i + 4, :], x_v[:, 4 * i:4 * i + 4, :]).then_inc(x_loaded, 16)
                sp.dma_start(g["ident"][:, :], io["c_ident"]).then_inc(x_loaded, 16)
                sp.wait_ge(x_loaded, 80)
        normalise_stats(nc, g["x"], g["norm"], None, 0, "n0")
        with ExitStack() as s0:
            m0 = Mem(nc, s0, "l0")
            g["qT"] = m0.sb("qT", [P, NT, 2, R0 * P], F32R)
            g["kT"] = m0.sb("kT", [P, 2, TOK], F32R)
            g["V"] = m0.sb("V", [P, NT, G0, HD + 1])
            g["queue"] = m0.sb("queue", [E0, TOK])
            g["logits"] = m0.sb("logits", [P, NT, E0])
            project0(nc, io, g)
            if upto >= 2:
                routing0(nc, io, g)
            if upto >= 3:
                attention0(nc, io, g)
        if upto >= 4:
            with ExitStack() as s1:
                m1 = Mem(nc, s1, "w1")
                g["up1"] = m1.sb("up1", [P, E1 + 1, KD, 2 * F1])
                g["down1"] = m1.sb("down1", [P, E1 + 1, F1 // P, D])
                g["weights1_in"] = m1.sem("weights1_in")
                g["weights1_n"] = 16 * 2 * (E1 * KD + 1)
                experts0(nc, io, g)
                combine0(nc, g)
                normalise_stats(nc, g["x"], g["norm"], None, 0, "n1")
                project1(nc, io, g)
                routing1(nc, io, g)
                if upto >= 6:
                    experts1(nc, io, g)
            gather1(nc, g)
        if upto >= 7:
            attention1(nc, io, g, out)


def layouts(inputs):
    a = {name: np.asarray(value) for name, value in inputs.items()}
    t = lambda name: np.ascontiguousarray(a[name].T)
    return {
        "x": a["L0_attn_x"].reshape(TOK, D),
        "Wq0": paired_heads(a["L0_attn_Wq"]),
        "Wkv0": a["L0_attn_Wkv"],
        "bq0": paired_heads(a["L0_attn_bq"]),
        "bkv0": a["L0_attn_bkv"].reshape(1, -1),
        "Wo0": a["L0_attn_Wo"],
        "bo0": a["L0_attn_bo"].reshape(1, -1),
        "routerT0": t("L0_ffn_router_weight"),
        "gate_up0": a["L0_ffn_gate_up_proj"],
        "down0": a["L0_ffn_down_proj"],
        "slope1": a["L1_attn_slope_rate"].reshape(1, H1),
        "norm1T": np.ascontiguousarray(a["L1_attn_norm_w"].reshape(H1, DH1).T),
        "WoT1": t("L1_attn_Wo"),
        "Wh1": head_weights(a["L1_attn_Wqkv"], a["L1_attn_Wg"]),
        "routerT1": t("L1_ffn_router_w"),
        "gate_up1": a["L1_ffn_w_gate_up"],
        "down1": a["L1_ffn_w_down"],
        "shared_up1": a["L1_ffn_shared_gate_up"],
        "shared_down1": a["L1_ffn_shared_down"],
        **layer0_constants(),
        **layer1_constants(),
    }


def kernel(**inputs):
    from concourse import bacc
    from concourse.bass_utils import run_bass_kernel_spmd

    nc = bacc.Bacc("TRN2", target_bir_lowering=False, num_devices=1)
    arrays, io = {}, {}
    for name, value in layouts(inputs).items():
        arrays[f"in_{name}"] = np.ascontiguousarray(value)
        io[name] = nc.dram_tensor(f"in_{name}", value.shape, mybir.dt.from_np(value.dtype), kind="ExternalInput").ap()
    out = nc.dram_tensor("out_y", (TOK, D), F32, kind="ExternalOutput").ap()
    program(nc, io, out)
    result = run_bass_kernel_spmd(nc, [arrays], core_ids=[0])
    return result.results[0]["out_y"].reshape(BATCH, SEQ, D)
```
